# Optimizing a Trainium2 kernel written in Bass

```python
import numpy as np
import jax
import jax.numpy as jnp

def _softmax(x, axis=-1):
    return jax.nn.softmax(x, axis=axis)

def _gelu(x):
    return jax.nn.gelu(x, approximate=True)

def _silu(x):
    return jax.nn.silu(x)

def _sigmoid(x):
    return jax.nn.sigmoid(x)

def _layernorm(x, axis=-1, eps=1e-05):
    m = jnp.mean(x, axis=axis, keepdims=True)
    v = jnp.var(x, axis=axis, keepdims=True)
    return (x - m) / jnp.sqrt(v + eps)

def _scatter_add(tgt, idx, src, axis=0):
    return tgt.at[idx].add(src)

def _segment_sum(src, seg, n):
    return jax.ops.segment_sum(src, seg, n)
kernel_name = 'mk_adj_resnorm_d2_adj_r2_4a912c'

def setup_inputs(seed: int=0):
    np.random.seed(seed)
    _w = jnp.asarray

    def _rec_inputs():
        import jax
        import jax.numpy as jnp
        _gk = jax.random.key(seed)
        x = 0.0001732 + 1 * jax.random.normal(jax.random.fold_in(_gk, 1), (5120, 64), jnp.float32)
        _a = jax.random.bernoulli(jax.random.fold_in(_gk, 2), 0.003125, (5120, 5120))
        _a = jnp.logical_or(_a, jnp.swapaxes(_a, -1, -2))
        _a = jnp.logical_or(_a, jnp.eye(5120, dtype=bool))
        _af = _a.astype(jnp.float32)
        _af = _af * jax.random.uniform(jax.random.fold_in(_gk, 3), (5120, 5120), jnp.float32, 0.05, 0.02)
        adj = _af
        return (x, adj)
    x, adj = _rec_inputs()

    def _L0_gnn_setup():
        import jax, jax.numpy as jnp
        import numpy as np
        N_USERS = 2048
        N_ITEMS = 3072
        EMB = 64
        LN_EPS = 1e-05
        key = jax.random.key(seed)
        ks = jax.random.split(key, 10)
        N = N_USERS + N_ITEMS
        ego = jax.random.normal(ks[0], (N, EMB), jnp.float32)
        adj = (jax.random.uniform(ks[1], (N, N), jnp.float32) < 0.01).astype(jnp.float32) * 0.02
        xav = float(np.sqrt(6.0 / (EMB + EMB)))
        W_u = jax.random.uniform(ks[2], (EMB, EMB), jnp.float32, -xav, xav)
        W_i = jax.random.uniform(ks[3], (EMB, EMB), jnp.float32, -xav, xav)
        diag_u = jax.random.uniform(ks[4], (N_USERS,), jnp.float32, 0.99, 1.01)
        diag_i = jax.random.uniform(ks[5], (N_ITEMS,), jnp.float32, 0.99, 1.01)
        par_u = jax.random.uniform(ks[6], (2,), jnp.float32, 0.0, 0.99)
        par_i = jax.random.uniform(ks[7], (2,), jnp.float32, 0.0, 0.99)
        ln_gamma = jnp.ones((EMB,), jnp.float32)
        ln_beta = jnp.zeros((EMB,), jnp.float32)
        return {'ego_embeddings': ego, 'adj': adj, 'W_u': W_u, 'diag_u': diag_u, 'par_u': par_u, 'W_i': W_i, 'diag_i': diag_i, 'par_i': par_i, 'ln_gamma': ln_gamma, 'ln_beta': ln_beta}
    _L0_gnn_all = _L0_gnn_setup()
    _L0_gnn_in = {k: v for k, v in _L0_gnn_all.items() if k in ('W_u', 'diag_u', 'par_u', 'W_i', 'diag_i', 'par_i', 'ln_gamma', 'ln_beta')}
    del _L0_gnn_all

    def _L1_gnn_setup():
        import jax, jax.numpy as jnp
        import numpy as np
        N, D, H = (8192, 64, 128)
        GAIN = 0.2
        key = jax.random.key(seed)
        ks = jax.random.split(key, 6)
        X = jax.random.normal(ks[0], (N, D), dtype=jnp.float32)
        t = jax.random.uniform(ks[1], (1,), dtype=jnp.float32)
        Wt = jax.random.uniform(ks[2], (N, N), dtype=jnp.float32)
        B = GAIN * jnp.eye(D, dtype=jnp.float32) + 0.01 * jax.random.normal(ks[3], (D, D), dtype=jnp.float32)
        W1 = jax.random.normal(ks[4], (D + 1, H), dtype=jnp.float32) * (1.0 / np.sqrt(D + 1))
        b1 = jnp.zeros((H,), dtype=jnp.float32)
        W2 = jax.random.normal(ks[5], (H, D), dtype=jnp.float32) * (1.0 / np.sqrt(H))
        b2 = jnp.zeros((D,), dtype=jnp.float32)
        return {'X': X, 't': t, 'Wt': Wt, 'B': B, 'W1': W1, 'b1': b1, 'W2': W2, 'b2': b2}
    _L1_gnn_all = _L1_gnn_setup()
    _L1_gnn_in = {k: v for k, v in _L1_gnn_all.items() if k in ('t', 'B', 'W1', 'b1', 'W2', 'b2')}
    del _L1_gnn_all
    return {'x': x, 'adj': adj, 'L0_gnn_W_u': _L0_gnn_in['W_u'], 'L0_gnn_diag_u': _L0_gnn_in['diag_u'], 'L0_gnn_par_u': _L0_gnn_in['par_u'], 'L0_gnn_W_i': _L0_gnn_in['W_i'], 'L0_gnn_diag_i': _L0_gnn_in['diag_i'], 'L0_gnn_par_i': _L0_gnn_in['par_i'], 'L0_gnn_ln_gamma': _L0_gnn_in['ln_gamma'], 'L0_gnn_ln_beta': _L0_gnn_in['ln_beta'], 'L1_gnn_t': _L1_gnn_in['t'], 'L1_gnn_B': _L1_gnn_in['B'], 'L1_gnn_W1': _L1_gnn_in['W1'], 'L1_gnn_b1': _L1_gnn_in['b1'], 'L1_gnn_W2': _L1_gnn_in['W2'], 'L1_gnn_b2': _L1_gnn_in['b2']}

def reference(x, adj, L0_gnn_W_u, L0_gnn_diag_u, L0_gnn_par_u, L0_gnn_W_i, L0_gnn_diag_i, L0_gnn_par_i, L0_gnn_ln_gamma, L0_gnn_ln_beta, L1_gnn_t, L1_gnn_B, L1_gnn_W1, L1_gnn_b1, L1_gnn_W2, L1_gnn_b2):
    import jax
    import jax.numpy as jnp

    def _L0_gnn_ref(ego_embeddings, adj, W_u, diag_u, par_u, W_i, diag_i, par_i, ln_gamma, ln_beta):
        import jax, jax.numpy as jnp
        import numpy as np
        N_USERS = 2048
        N_ITEMS = 3072
        EMB = 64
        LN_EPS = 1e-05
        nu = diag_u.shape[0]
        res = ego_embeddings
        ego_u = ego_embeddings[:nu]
        ego_i = ego_embeddings[nu:]
        u = par_u[0] * par_u[1] * (diag_u[:, None] * ego_u @ W_u) + ego_u
        i = par_i[0] * par_i[1] * (diag_i[:, None] * ego_i @ W_i) + ego_i
        e = jnp.concatenate([u, i], axis=0)
        h = adj @ (adj.T @ e)
        mu = jnp.mean(h, axis=-1, keepdims=True)
        var = jnp.var(h, axis=-1, keepdims=True)
        out = (h - mu) * jax.lax.rsqrt(var + LN_EPS) * ln_gamma + ln_beta + res
        return out

    def _L1_gnn_ref(X, t, Wt, B, W1, b1, W2, b2):
        import jax, jax.numpy as jnp
        import numpy as np
        N, D, H = (8192, 64, 128)
        GAIN = 0.2
        n = X.shape[0]
        tcol = jnp.broadcast_to(t.reshape(1, 1), (n, 1))
        h = jnp.tanh(jnp.concatenate([X, tcol], axis=1) @ W1 + b1)
        u_intra = h @ W2 + b2
        XB = X @ B.T
        u_comm = Wt @ XB - jnp.sum(Wt, axis=1, keepdims=True) * XB
        return u_intra + u_comm
    x = _layernorm(x + _L0_gnn_ref(x, adj, L0_gnn_W_u, L0_gnn_diag_u, L0_gnn_par_u, L0_gnn_W_i, L0_gnn_diag_i, L0_gnn_par_i, L0_gnn_ln_gamma, L0_gnn_ln_beta), axis=-1)
    x = _layernorm(x + _L1_gnn_ref(x, L1_gnn_t, adj, L1_gnn_B, L1_gnn_W1, L1_gnn_b1, L1_gnn_W2, L1_gnn_b2), axis=-1)
    return x

_drawn_inputs = setup_inputs


def setup_inputs(seed=0):
    import zlib

    import numpy as np

    out = dict(_drawn_inputs(seed))
    spreads = {'L0_gnn_ln_gamma': (1.0, 0.2),
     'L0_gnn_ln_beta': (0.0, 0.1),
     'L1_gnn_b1': (0.0, 0.1),
     'L1_gnn_b2': (0.0, 0.1)}
    factors = {'L0_gnn_diag_u': 8.0, 'L0_gnn_W_i': 5.295, 'L0_gnn_diag_i': 8.0}
    for name, (base, spread) in spreads.items():
        noise = np.random.default_rng([zlib.crc32(name.encode()), seed]).standard_normal(out[name].shape)
        drawn = base * np.exp(spread * noise) if base else spread * noise
        out[name] = jnp.asarray(drawn.astype(out[name].dtype))
    for name, factor in factors.items():
        out[name] = (out[name] * factor).astype(out[name].dtype)
    return out
```

```python
from contextlib import ExitStack

import concourse.bass as bass
from concourse import mybir

F32 = mybir.dt.float32
F32R = mybir.dt.float32r
ALU = mybir.AluOpType
ACT = mybir.ActivationFunctionType
AX = mybir.AxisListType

P = 128
D = 64
N = 5120
T = N // P
H = 128
USERS = 2048
LN_EPS = 1e-5

W = 256
NB = N // W
CH = W // P
G = 4
NG = T // G
RAW = 5
NAT = 2
DOUBLE = 3
P2_AFTER = {3: [0], 4: [1, 2], 5: [3], **{2 * g - 1: [g] for g in range(4, NG)}}
ADD_AFTER = {3: [0], 4: [1, 2, 3], 5: [4], 6: [5], 7: [6], 8: [7], 9: [8, 9]}

BT = 8
NBATCH = T // BT

PIECES = 4
PW = N // PIECES
KP = PW // P
STAGE = 4
TB = 4
LAG = 2
FOLD_ROWS = 2

BANK_YT, BANK_Y = 0, 1
BANK_T = 2
BANK_P2 = 6
BANK_ACC, BANK_OUT = 0, 1


def build(nc, x, adj, W_u, diag_u, par_u, W_i, diag_i, par_i, ln_gamma, ln_beta, t, B, W1, b1, W2, b2, out):
    ctx = ExitStack()
    with ctx:
        def sb(name, shape, dt=F32, scope=ctx):
            return scope.enter_context(nc.sbuf_tensor(name, shape, dt))

        def sem(name):
            return ctx.enter_context(nc.semaphore(name))

        ps = ctx.enter_context(nc.psum_tensor("ps", [P, 8, 512], F32))

        ident = sb("ident", [P, P])
        ident_r = sb("ident_r", [P, P], F32R)
        X = sb("X", [P, T, D])
        stat = sb("stat", [P, T, 2 * D], F32R)
        hT = sb("hT", [P, N])
        diag = sb("diag", [P, T])
        wu = sb("wu", [D, D])
        wi = sb("wi", [D, D])
        pars = sb("pars", [P, 4])
        pp = sb("pp", [P, 2])
        gam = sb("gam", [P, D])
        bet = sb("bet", [P, D])
        b2r = sb("b2r", [P, D])
        BTs = sb("BTs", [D, D])
        w1 = sb("w1", [D, H])
        w1t = sb("w1t", [P, 1])
        b1c = sb("b1c", [P, 1])
        tc = sb("tc", [P, 1])
        hbias = sb("hbias", [P, 1])
        w2 = sb("w2", [H, D])
        minus_half = sb("minus_half", [P, BT])

        hid = sb("hid", [P, BT * P])
        accT = hid[:, 0:G * P]
        dump = hT[:, 0:2 * PW].rearrange("p (a c) -> p a c", a=2)

        with ExitStack() as first:
            AT = sb("AT", [P, NG + DOUBLE, 2, CH, G * P], F32R, first)
            raw = sb("raw", [P, RAW, G, W], scope=first)
            nat_hi = sb("nat_hi", [P, NAT, G, W], F32R, first)
            nat_lo = sb("nat_lo", [P, NAT, G, W], F32R, first)
            yT = sb("yT", [P, W], scope=first)
            yf = sb("yf", [P, CH, D], scope=first)
            ystat = sb("ystat", [P, CH, 2 * D], F32R, first)

        with ExitStack() as before:
            xs = sb("xs", [P, 2, BT, D], scope=before)
            xsT = sb("xsT", [D, 2, BT * P], scope=before)
            ef = sb("ef", [P, 2, BT * D], scope=before)

        with ExitStack() as second:
            raw2 = sb("raw2", [P, PIECES, G, PW], scope=second)
            s_hi = sb("s_hi", [P, STAGE, G * P], F32R, second)
            s_lo = sb("s_lo", [P, STAGE, G * P], F32R, second)
            f1 = sb("f1", [P, FOLD_ROWS, PW // 2], scope=second)
            f2 = sb("f2", [P, FOLD_ROWS, PW // 4], scope=second)
            f3 = sb("f3", [P, FOLD_ROWS, PW // 8], scope=second)
            Z = sb("Z", [P, T, D], scope=second)
            R = sb("R", [P, T, D], scope=second)
            hc = sb("hc", [P, 2, BT, D], scope=second)
            sq = sb("sq", [P, BT, D], scope=second)
            st = sb("st", [P, 5, BT], scope=second)
            x1 = sb("x1", [P, 2, BT, D], scope=second)
            x1b = sb("x1b", [P, BT, D], scope=second)
            xT = sb("xT", [D, BT * P], scope=second)
            rsp = sb("rsp", [P, T, PIECES], scope=second)
            rst = sb("rst", [P, G], scope=second)
            o = sb("o", [P, G, D], scope=second)
            oz = sb("oz", [P, G, D], scope=second)
            osq = sb("osq", [P, G, D], scope=second)
            ost = sb("ost", [P, 3, G], scope=second)

        consts_in = sem("consts_in")
        x_in = sem("x_in")
        raw_in = [sem(f"raw_in{s}") for s in range(RAW)]
        id_zero, id_made, id_round = sem("id_zero"), sem("id_made"), sem("id_round")
        pp_made, hb_made = sem("pp_made"), sem("hb_made")
        xs_made, xs_turned, xsT_copied, e_mm, e_made = (sem(n) for n in ("xs_made", "xs_turned", "xsT_copied", "e_mm", "e_made"))
        e_sum, e_hi = sem("e_sum"), sem("e_hi")
        x_doubled, base_made = sem("x_doubled"), sem("base_made")
        hT_zeroed = sem("hT_zeroed")
        hi_ready, lo_ready = sem("hi_ready"), sem("lo_ready")
        t_done, at_ready = sem("t_done"), sem("at_ready")
        p1_done, yT_copied, y_turned = sem("p1_done"), sem("yT_copied"), sem("y_turned")
        y_sum, y_hi, y_ready = sem("y_sum"), sem("y_hi"), sem("y_ready")
        p2_done, h_added = sem("p2_done"), sem("h_added")
        h_turned, ln_link, hn_read, x1_ready = sem("h_turned"), sem("ln_link"), sem("hn_read"), sem("x1_ready")
        var_ready, rstd_ready, orstd_ready, var_eps, half_made = (
            sem(n) for n in ("var_ready", "rstd_ready", "orstd_ready", "var_eps", "half_made"))
        x1_turned, xT_copied, z_mm, hid_mm, hid_made, u_mm = (sem(n) for n in ("x1_turned", "xT_copied", "z_mm", "hid_mm", "hid_made", "u_mm"))
        x1b_made, z_copied, z_hi, z_ready, r_ready = (sem(n) for n in ("x1b_made", "z_copied", "z_hi", "z_ready", "r_ready"))
        raw2_in = [sem(f"raw2_in{c}") for c in range(PIECES)]
        t2_done, hi2_ready, lo2_ready, p3_done = sem("t2_done"), sem("hi2_ready"), sem("lo2_ready"), sem("p3_done")
        turned, fold1, fold2, fold3, fold_summed = (sem(n) for n in ("turned", "fold1", "fold2", "fold3", "fold_summed"))
        act_summed = [sem(f"act_summed{r}") for r in range(FOLD_ROWS, G)]
        acc_copied, o_turned, epi_link = sem("acc_copied"), sem("o_turned"), sem("epi_link")
        stored = sem("stored")

        adj_cols = adj.rearrange("(g r p) c -> p g r c", r=G, p=P)
        out_v = out.rearrange("(t p) d -> p t d", p=P)
        x_v = x.rearrange("(t p) d -> p t d", p=P)
        UT = USERS // P
        CONSTS = 15
        RSTD_SCALE = float(D) ** 0.5
        EPI = 11

        def slot_of(J, g):
            if g >= DOUBLE:
                return g
            return g + NG * (J % 2)

        block = ctx.enter_context(nc.Block())

        @block.sync
        def _(sp):
            sp.dma_start(X[:, :, :], x_v).then_inc(x_in, 16)

            def load_block(J, peeled):
                first_col = J * W if peeled else sp.snap(J * W)
                for g in range(NG):
                    s = g % RAW
                    if not peeled or g >= RAW:
                        sp.wait_ge(lo_ready, NG * J + g - RAW + 1)
                    sp.dma_start(raw[:, s, :, :], adj_cols[:, g, :, bass.ds(first_col, W)]).then_inc(raw_in[s], 16)

            load_block(0, True)
            with sp.Fori(1, NB) as J:
                load_block(J, False)

            def load_piece(m, c):
                sp.dma_start(raw2[:, c, :, :], adj_cols[:, m, :, c * PW:(c + 1) * PW]).then_inc(raw2_in[c], 16)

            def store(m):
                first_tile = sp.snap(m * G) if not isinstance(m, int) else m * G
                sp.wait_ge(epi_link, EPI * (m + 1))
                sp.dma_start(out_v[:, bass.ds(first_tile, G), :], R[:, bass.ds(first_tile, G), :]).then_inc(stored, 16)

            sp.wait_ge(p2_done, NB * NG)
            for c in range(PIECES):
                load_piece(0, c)

            def load_group(m):
                for c in range(PIECES):
                    n = PIECES * (m - 1) + c
                    sp.wait_ge(turned, n + 1)
                    sp.wait_ge(fold1, n + 1)
                    for summed in act_summed:
                        sp.wait_ge(summed, n + 1)
                    load_piece(m, c)

            load_group(1)
            with sp.Fori(2, NG) as m:
                load_group(m)
                store(m - 2)
            store(NG - 2)
            store(NG - 1)
            sp.wait_ge(stored, 16 * NG)

        @block.scalar
        def _(act):
            with nc.allow_non_contiguous_dma("small constants, once"):
                for dst, src in (
                    (diag[:, 0:UT], diag_u.rearrange("(t p) -> p t", p=P)),
                    (diag[:, UT:T], diag_i.rearrange("(t p) -> p t", p=P)),
                    (wu[:, :], W_u), (wi[:, :], W_i),
                    (pars[:, 0:2], par_u.partition_broadcast(P)),
                    (pars[:, 2:4], par_i.partition_broadcast(P)),
                    (gam[:, :], ln_gamma.partition_broadcast(P)),
                    (bet[:, :], ln_beta.partition_broadcast(P)),
                    (b2r[:, :], b2.partition_broadcast(P)),
                    (BTs[:, :], B.rearrange("o d -> d o")),
                    (w1[:, :], W1[0:D, :]),
                    (w1t[:, :], W1[D:D + 1, :].rearrange("a h -> h a")),
                    (b1c[:, :], b1.rearrange("(h a) -> h a", a=1)),
                    (tc[:, :], t.partition_broadcast(P)),
                    (w2[:, :], W2),
                ):
                    act.dma_start(dst, src).then_inc(consts_in, 16)

            for b in range(NBATCH):
                act.wait_ge(xs_turned, b + 1)
                if b >= 2:
                    act.wait_ge(e_mm, b - 1)
                act.copy(xsT[:, b % 2, :], ps[0:D, BANK_T + 2:BANK_T + 4, :].rearrange("p a c -> p (a c)")).then_inc(xsT_copied, 1)

            def copy_yT(J):
                act.wait_ge(p1_done, NG * J)
                act.copy(yT[:, :], ps[:, BANK_YT, 0:W]).then_inc(yT_copied, 1)

            def keep_tiles(J, peeled):
                for g in range(NG):
                    for half in range(2):
                        u = 2 * (NG * J + g) + half
                        act.wait_ge(t_done, u + 1)
                        if not peeled and half == 0:
                            if g >= DOUBLE:
                                act.wait_ge(p2_done, NG * (J - 1) + g + 1)
                            else:
                                act.wait_ge(y_turned, J)
                        b0 = BANK_T + 2 * half
                        dst = AT[:, slot_of(J, g), :, :, half * 2 * P:(half + 1) * 2 * P]
                        act.copy(dst.rearrange("p h k (r i) -> p r (h k) i", r=2),
                                 ps[:, b0:b0 + 2, :].rearrange("p r (q i) -> p r q i", i=P)).then_inc(at_ready, 1)

            keep_tiles(0, True)
            with act.Fori(1, NB) as J:
                copy_yT(J)
                keep_tiles(J, False)
            copy_yT(NB)

            for b in range(NBATCH):
                act.wait_ge(x1_turned, b + 1)
                if b >= 1:
                    act.wait_ge(z_mm, b)
                    act.wait_ge(hid_mm, b)
                act.copy(xT[:, :], ps[0:D, BANK_T + 2:BANK_T + 4, :].rearrange("p a c -> p (a c)")).then_inc(xT_copied, 1)
                act.wait_ge(hid_mm, b + 1)
                if b == 0:
                    act.wait_ge(hb_made, 1)
                if b >= 1:
                    act.wait_ge(u_mm, b)
                act.activation(hid[:, :], ps[:, BANK_T + 2:BANK_T + 4, :].rearrange("p a c -> p (a c)"), ACT.Tanh,
                               bias=hbias[:, 0:1]).then_inc(hid_made, 1)

            def copy_acc(m):
                act.wait_ge(p3_done, T * m)
                act.copy(accT, ps[:, BANK_ACC, :]).then_inc(acc_copied, 1)

            def split_hi(m, peeled):
                for k in range(T):
                    v = T * m + k
                    act.wait_ge(t2_done, v + 1)
                    if not peeled or k >= STAGE:
                        act.wait_ge(p3_done, v - STAGE + 1)
                    act.copy(s_hi[:, k % STAGE, :], ps[:, BANK_T + k % TB, :]).then_inc(hi2_ready, 1)
                    c = k // KP
                    if k % KP in (3, 7):
                        q = (k % KP - 3) // 4
                        r = FOLD_ROWS + q
                        if q == 0:
                            act.wait_ge(raw2_in[c], 16 * (m + 1))
                        if not peeled or c:
                            act.wait_ge(act_summed[q], PIECES * m + c)
                        act.activation(dump[:, q, :], raw2[:, c, r, :], ACT.Copy,
                                       accum_out=rsp[:, bass.ds(m * G + r, 1), c]).then_inc(act_summed[q], 1)

            act.wait_ge(r_ready, NBATCH)
            split_hi(0, True)
            with act.Fori(1, NG) as m:
                copy_acc(m)
                split_hi(m, False)
            copy_acc(NG)

        @block.gpsimd
        def _(pool):
            pool.memset(ident[:, :], 0.0).then_inc(id_zero, 1)
            pool.wait_ge(id_zero, 1)
            pool.affine_select(out=ident[:, :], in_=ident[:, :], compare_op=ALU.not_equal, fill=1.0, base=0,
                               pattern=[[-1, P]], channel_multiplier=1).then_inc(id_made, 1)
            pool.memset(minus_half[:, :], -0.5).then_inc(half_made, 1)
            pool.memset(hT[:, :], 0.0).then_inc(hT_zeroed, 1)
            pool.wait_ge(consts_in, 16 * CONSTS)
            pool.wait_ge(e_made, NBATCH)
            pool.tensor_tensor(X[:, :, :], X[:, :, :], X[:, :, :], ALU.add).then_inc(x_doubled, 1)
            pool.wait_ge(x_doubled, 1)
            pool.tensor_tensor(X[:, :, :], X[:, :, :], bet[:, :].unsqueeze(1).to_broadcast([P, T, D]),
                               ALU.add).then_inc(base_made, 1)

            def rstd(k):
                pool.wait_ge(var_ready, k + 1)
                pool.tensor_scalar(st[:, 1 + k % 2, :], st[:, 1 + k % 2, :], LN_EPS * D, None, ALU.add).then_inc(var_eps, 1)
                pool.wait_ge(var_eps, k + 1)
                pool.tensor_tensor(st[:, 3 + k % 2, :], st[:, 1 + k % 2, :], minus_half[:, :], ALU.pow).then_inc(rstd_ready, 1)

            def add_b2(b):
                pool.wait_ge(x1_ready, b + 1)
                if b >= 1:
                    pool.wait_ge(r_ready, b)
                pool.tensor_tensor(x1b[:, :, :], x1[:, b % 2, :, :], b2r[:, :].unsqueeze(1).to_broadcast([P, BT, D]),
                                   ALU.add).then_inc(x1b_made, 1)

            pool.wait_ge(half_made, 1)
            for b in range(NBATCH):
                rstd(2 * b)
                if b:
                    add_b2(b - 1)
                rstd(2 * b + 1)
            add_b2(NBATCH - 1)

            def rstd_of_out(m):
                pool.wait_ge(epi_link, EPI * m + EPI - 1)
                pool.tensor_tensor(ost[:, 2, :], ost[:, 1, :], minus_half[:, 0:G], ALU.pow).then_inc(orstd_ready, 1)

            def fold(m, peeled):
                for c in range(PIECES):
                    if not peeled and c == PIECES - 1:
                        rstd_of_out(m - 1)
                    n = PIECES * m + c
                    q = PW // 2
                    pool.wait_ge(raw2_in[c], 16 * (m + 1))
                    if not peeled or c:
                        pool.wait_ge(fold2, n)
                    pool.tensor_tensor(f1[:, :, :], raw2[:, c, 0:FOLD_ROWS, 0:q], raw2[:, c, 0:FOLD_ROWS, q:2 * q],
                                       ALU.add).then_inc(fold1, 1)
                    pool.wait_ge(fold1, n + 1)
                    if not peeled or c:
                        pool.wait_ge(fold3, n)
                    q //= 2
                    pool.tensor_tensor(f2[:, :, :], f1[:, :, 0:q], f1[:, :, q:2 * q], ALU.add).then_inc(fold2, 1)
                    pool.wait_ge(fold2, n + 1)
                    if not peeled or c:
                        pool.wait_ge(fold_summed, n)
                    q //= 2
                    pool.tensor_tensor(f3[:, :, :], f2[:, :, 0:q], f2[:, :, q:2 * q], ALU.add).then_inc(fold3, 1)

            fold(0, True)
            with pool.Fori(1, NG) as m:
                fold(m, False)
            rstd_of_out(NG - 1)

        @block.vector
        def _(dve):
            dve.wait_ge(id_made, 1)
            dve.tensor_copy(ident_r[:, :], ident[:, :]).then_inc(id_round, 1)
            dve.wait_ge(consts_in, 16 * CONSTS)
            dve.tensor_tensor(pp[:, :], pars[:, 0:4:2], pars[:, 1:4:2], ALU.mult).then_inc(pp_made, 1)
            dve.scalar_tensor_tensor(hbias[:, :], w1t[:, :], tc[:, 0:1], b1c[:, :], ALU.mult, ALU.add).then_inc(hb_made, 1)
            dve.wait_ge(x_in, 16)

            def scale_x(b):
                if b >= 2:
                    dve.wait_ge(xs_turned, b - 1)
                dve.tensor_tensor(xs[:, b % 2, :, :], X[:, b * BT:(b + 1) * BT, :],
                                  diag[:, b * BT:(b + 1) * BT].unsqueeze(2).to_broadcast([P, BT, D]),
                                  ALU.mult).then_inc(xs_made, 1)

            def make_e(b):
                who = 0 if b * BT < UT else 1
                dve.wait_ge(e_mm, b + 1)
                if b == 0:
                    dve.wait_ge(pp_made, 1)
                e = ef[:, b % 2, :]
                dve.scalar_tensor_tensor(e, ps[:, BANK_P2 + b % 2, :], pp[:, who:who + 1],
                                         X[:, b * BT:(b + 1) * BT, :].rearrange("p t d -> p (t d)"),
                                         ALU.mult, ALU.add).then_inc(e_sum, 1)
                dve.wait_ge(e_sum, b + 1)
                dst = stat[:, b * BT:(b + 1) * BT, :]
                ev = e.rearrange("p (t d) -> p t d", d=D)
                dve.tensor_copy(dst[:, :, 0:D], ev).then_inc(e_hi, 1)
                dve.wait_ge(e_hi, b + 1)
                dve.tensor_tensor(dst[:, :, D:2 * D], ev, dst[:, :, 0:D].bitcast(F32), ALU.subtract).then_inc(e_made, 1)

            scale_x(0)
            scale_x(1)
            for b in range(NBATCH):
                make_e(b)
                if b + 2 < NBATCH:
                    scale_x(b + 2)

            def split(J, g, peeled):
                n = NG * J + g
                s = g % RAW
                dve.wait_ge(raw_in[s], 16 * (NG // RAW * J + g // RAW + 1))
                if not peeled or g >= NAT:
                    dve.wait_ge(p1_done, n - NAT + 1)
                dve.tensor_copy(nat_hi[:, g % NAT, :, :], raw[:, s, :, :]).then_inc(hi_ready, 1)
                dve.wait_ge(hi_ready, n + 1)
                dve.tensor_tensor(nat_lo[:, g % NAT, :, :], raw[:, s, :, :], nat_hi[:, g % NAT, :, :].bitcast(F32),
                                  ALU.subtract).then_inc(lo_ready, 1)

            def make_y(J):
                dve.wait_ge(y_turned, J)
                yv = ps[:, BANK_Y, 0:CH * P].rearrange("p (k c) -> p k c", c=P)
                dve.tensor_copy(yf[:, :, :], yv[:, :, 0:D]).then_inc(y_sum, 1)
                dve.wait_ge(y_sum, 2 * J - 1)
                dve.tensor_tensor(yf[:, :, :], yf[:, :, :], yv[:, :, D:2 * D], ALU.add).then_inc(y_sum, 1)
                dve.wait_ge(y_sum, 2 * J)
                dve.tensor_copy(ystat[:, :, 0:D], yf[:, :, :]).then_inc(y_hi, 1)
                dve.wait_ge(y_hi, J)
                dve.tensor_tensor(ystat[:, :, D:2 * D], yf[:, :, :], ystat[:, :, 0:D].bitcast(F32),
                                  ALU.subtract).then_inc(y_ready, 1)

            def add_h(J, g):
                dve.wait_ge(p2_done, NG * (J - 1) + g + 1)
                cols = hT[:, g * G * P:(g + 1) * G * P]
                dve.tensor_tensor(cols, cols, ps[:, BANK_P2 + g % 2, :], ALU.add).then_inc(h_added, 1)

            for g in range(NG):
                split(0, g, True)
            dve.wait_ge(hT_zeroed, 1)
            with dve.Fori(1, NB) as J:
                for g in range(NG):
                    split(J, g, False)
                    if g == 1:
                        make_y(J)
                    for g2 in ADD_AFTER.get(g, []):
                        add_h(J, g2)
            make_y(NB)

            links = [0]

            def link(ins):
                links[0] += 1
                ins.then_inc(ln_link, 1)
                dve.wait_ge(ln_link, links[0])

            def inner_sum(dst, src):
                return dve.tensor_reduce(dst, src, AX.X, ALU.add)

            def spread(h, k):
                link(inner_sum(st[:, 0, :], h))
                link(dve.scalar_tensor_tensor(h, st[:, 0, :].unsqueeze(2).to_broadcast([P, BT, D]), 1.0 / D, h,
                                              ALU.mult, ALU.subtract))
                link(dve.tensor_tensor(sq[:, :, :], h, h, ALU.mult))
                if k >= 2:
                    dve.wait_ge(rstd_ready, k - 1)
                inner_sum(st[:, 1 + k % 2, :], sq[:, :, :]).then_inc(var_ready, 1)
                dve.wait_ge(var_ready, k + 1)

            def normalised(dst, h, k):
                dve.wait_ge(rstd_ready, k + 1)
                return dve.scalar_tensor_tensor(dst, h, -RSTD_SCALE, st[:, 3 + k % 2, :].unsqueeze(2).to_broadcast([P, BT, D]),
                                                ALU.mult, ALU.mult)

            def start_ln1(b):
                h = hc[:, b % 2, :, :]
                dve.wait_ge(h_turned, b + 1)
                hv = ps[:, BANK_T:BANK_T + 2, :].rearrange("p a (t c) -> p (a t) c", c=P)
                link(dve.tensor_copy(h, hv[:, :, 0:D]))
                dve.tensor_tensor(h, h, hv[:, :, D:2 * D], ALU.add).then_inc(hn_read, 1)
                dve.wait_ge(hn_read, b + 1)
                spread(h, 2 * b)

            def start_ln2(b):
                h = hc[:, b % 2, :, :]
                link(normalised(h, h, 2 * b))
                link(dve.tensor_tensor(h, h, gam[:, :].unsqueeze(1).to_broadcast([P, BT, D]), ALU.mult))
                if b == 0:
                    dve.wait_ge(base_made, 1)
                link(dve.tensor_tensor(h, h, X[:, b * BT:(b + 1) * BT, :], ALU.add))
                spread(h, 2 * b + 1)

            def make_x1(b):
                if b >= 2:
                    dve.wait_ge(x1b_made, b - 1)
                normalised(x1[:, b % 2, :, :], hc[:, b % 2, :, :], 2 * b + 1).then_inc(x1_ready, 1)

            def make_zr(b):
                tiles = slice(b * BT, (b + 1) * BT)
                dve.wait_ge(z_mm, b + 1)
                dve.tensor_copy(Z[:, tiles, :], ps[:, BANK_ACC, :].rearrange("p (t d) -> p t d", d=D)).then_inc(z_copied, 1)
                dve.wait_ge(z_copied, b + 1)
                dve.tensor_copy(stat[:, tiles, 0:D], Z[:, tiles, :]).then_inc(z_hi, 1)
                dve.wait_ge(z_hi, b + 1)
                dve.tensor_tensor(stat[:, tiles, D:2 * D], Z[:, tiles, :], stat[:, tiles, 0:D].bitcast(F32),
                                  ALU.subtract).then_inc(z_ready, 1)
                dve.wait_ge(u_mm, b + 1)
                dve.wait_ge(x1b_made, b + 1)
                dve.tensor_tensor(R[:, tiles, :], ps[:, BANK_OUT, :].rearrange("p (t d) -> p t d", d=D),
                                  x1b[:, :, :], ALU.add).then_inc(r_ready, 1)

            for b in range(NBATCH + 2):
                if b < NBATCH:
                    add_h(NB, 2 * b)
                    add_h(NB, 2 * b + 1)
                    start_ln1(b)
                if 1 <= b <= NBATCH:
                    make_x1(b - 1)
                if b >= 2:
                    make_zr(b - 2)
                if b < NBATCH:
                    start_ln2(b)

            def epilogue(m, s):
                if s:
                    dve.wait_ge(epi_link, EPI * m + s)
                rows = bass.ds(m * G, G)
                wide = [P, G, D]
                if s == 0:
                    for summed in act_summed:
                        dve.wait_ge(summed, PIECES * (m + 1))
                    dve.wait_ge(fold_summed, PIECES * (m + 1))
                    ins = inner_sum(rst[:, :], rsp[:, rows, :])
                elif s == 1:
                    ins = dve.tensor_tensor(oz[:, :, :], Z[:, rows, :], rst[:, :].unsqueeze(2).to_broadcast(wide), ALU.mult)
                elif s == 2:
                    ins = dve.tensor_tensor(o[:, :, :], R[:, rows, :], oz[:, :, :], ALU.subtract)
                elif s in (3, 4):
                    dve.wait_ge(o_turned, m + 1)
                    half = ps[:, BANK_OUT, :].rearrange("p (r c) -> p r c", c=P)[:, :, (s - 3) * D:(s - 2) * D]
                    ins = dve.tensor_tensor(o[:, :, :], o[:, :, :], half, ALU.add)
                elif s == 5:
                    ins = inner_sum(ost[:, 0, :], o[:, :, :])
                elif s == 6:
                    ins = dve.scalar_tensor_tensor(o[:, :, :], ost[:, 0, :].unsqueeze(2).to_broadcast(wide), 1.0 / D,
                                                   o[:, :, :], ALU.mult, ALU.subtract)
                elif s == 7:
                    ins = dve.tensor_tensor(osq[:, :, :], o[:, :, :], o[:, :, :], ALU.mult)
                elif s == 8:
                    ins = inner_sum(ost[:, 1, :], osq[:, :, :])
                elif s == 9:
                    ins = dve.tensor_scalar(ost[:, 1, :], ost[:, 1, :], LN_EPS * D, None, ALU.add)
                else:
                    dve.wait_ge(orstd_ready, m + 1)
                    ins = dve.scalar_tensor_tensor(R[:, rows, :], o[:, :, :], -RSTD_SCALE,
                                                   ost[:, 2, :].unsqueeze(2).to_broadcast(wide), ALU.mult, ALU.mult)
                ins.then_inc(epi_link, 1)

            def split_lo(m, peeled):
                for k in range(T):
                    v = T * m + k
                    dve.wait_ge(hi2_ready, v + 1)
                    dve.tensor_tensor(s_lo[:, k % STAGE, :], ps[:, BANK_T + k % TB, :],
                                      s_hi[:, k % STAGE, :].bitcast(F32), ALU.subtract).then_inc(lo2_ready, 1)
                    if not peeled and 4 <= k and (k - 4) % 2 == 0 and (k - 4) // 2 < EPI:
                        epilogue(m - 1, (k - 4) // 2)
                    if k % KP == KP - 1:
                        c = k // KP
                        dve.wait_ge(fold3, PIECES * m + c + 1)
                        inner_sum(rsp[:, bass.ds(m * G, FOLD_ROWS), c], f3[:, :, :]).then_inc(fold_summed, 1)

            split_lo(0, True)
            with dve.Fori(1, NG) as m:
                split_lo(m, False)
            for s in range(EPI):
                epilogue(NG - 1, s)

        @block.tensor
        def _(pe):
            pe.wait_ge(id_made, 1)
            pe.wait_ge(consts_in, 16 * CONSTS)

            def turn_xs(b):
                pe.wait_ge(xs_made, b + 1)
                if b:
                    pe.wait_ge(xsT_copied, b)
                for r in range(BT):
                    ins = pe.transpose(ps[0:D, BANK_T + 2 + r // 4, (r % 4) * P:(r % 4 + 1) * P], xs[:, b % 2, r, :], ident[:, :])
                ins.then_inc(xs_turned, 1)

            def mm_e(b):
                pe.wait_ge(xsT_copied, b + 1)
                if b >= 2:
                    pe.wait_ge(e_sum, b - 1)
                w = wu if b * BT < UT else wi
                for r in range(BT):
                    ins = pe.matmul(ps[:, BANK_P2 + b % 2, r * D:(r + 1) * D], xsT[:, b % 2, r * P:(r + 1) * P], w[:, :],
                                    start=True, stop=True)
                ins.then_inc(e_mm, 1)

            turn_xs(0)
            for b in range(NBATCH):
                if b + 1 < NBATCH:
                    turn_xs(b + 1)
                mm_e(b)

            def turn_tiles(J, g, half, peeled):
                u = 2 * (NG * J + g) + half
                if not peeled or u >= 2:
                    pe.wait_ge(at_ready, u - 1)
                for r in (2 * half, 2 * half + 1):
                    for h, part in enumerate((nat_hi, nat_lo)):
                        for k in range(CH):
                            q = h * CH + k
                            ins = pe.transpose(ps[:, BANK_T + r, q * P:(q + 1) * P].bitcast(F32R),
                                               part[:, g % NAT, r, k * P:(k + 1) * P], ident_r[:, :])
                ins.then_inc(t_done, 1)

            def mm_y(J, g, half):
                for r in (2 * half, 2 * half + 1):
                    i = g * G + r
                    for part in (nat_hi, nat_lo):
                        ins = pe.matmul(ps[:, BANK_YT, 0:W], stat[:, i, :], part[:, g % NAT, r, :],
                                        start=(i == 0 and part is nat_hi), stop=(i == T - 1 and part is nat_lo))
                if half:
                    ins.then_inc(p1_done, 1)

            def turn_y(J):
                pe.wait_ge(yT_copied, J)
                for k in range(CH):
                    ins = pe.transpose(ps[:, BANK_Y, k * P:(k + 1) * P], yT[:, k * P:(k + 1) * P], ident[:, :])
                ins.then_inc(y_turned, 1)

            def mm_h(J, g):
                if g == 0:
                    pe.wait_ge(y_ready, J)
                pe.wait_ge(at_ready, 2 * (NG * (J - 1) + g + 1))
                if g >= 2:
                    pe.wait_ge(h_added, NG * (J - 1) + g - 1)
                for k in range(CH):
                    for h in range(2):
                        ins = pe.matmul(ps[:, BANK_P2 + g % 2, :], ystat[:, k, :], AT[:, slot_of(J - 1, g), h, k, :],
                                        start=(k == 0 and h == 0), stop=(k == CH - 1 and h == 1))
                ins.then_inc(p2_done, 1)

            def block_products(J, peeled):
                for g in range(NG):
                    pe.wait_ge(lo_ready, NG * J + g + 1)
                    if peeled and g % 2 == 0:
                        pe.wait_ge(e_made, g // 2 + 1)
                    for half in range(2):
                        turn_tiles(J, g, half, peeled)
                        if not peeled and g == 0 and half == 0:
                            turn_y(J)
                        mm_y(J, g, half)
                        if not peeled:
                            for g2 in P2_AFTER.get(2 * g + half, []):
                                mm_h(J, g2)

            pe.wait_ge(id_round, 1)
            block_products(0, True)
            with pe.Fori(1, NB) as J:
                block_products(J, False)
            turn_y(NB)

            def turn_h(b):
                pe.wait_ge(h_added, NG * (NB - 1) + 2 * b + 2)
                if b:
                    pe.wait_ge(hn_read, b)
                else:
                    pe.wait_ge(at_ready, 2 * NB * NG)
                for r in range(BT):
                    i = b * BT + r
                    ins = pe.transpose(ps[:, BANK_T + r // 4, (r % 4) * P:(r % 4 + 1) * P], hT[:, i * P:(i + 1) * P], ident[:, :])
                ins.then_inc(h_turned, 1)

            def mm_z(b):
                pe.wait_ge(x1_ready, b + 1)
                if b:
                    pe.wait_ge(hid_made, b)
                for r in range(BT):
                    ins = pe.transpose(ps[0:D, BANK_T + 2 + r // 4, (r % 4) * P:(r % 4 + 1) * P], x1[:, b % 2, r, :], ident[:, :])
                ins.then_inc(x1_turned, 1)
                pe.wait_ge(xT_copied, b + 1)
                if b:
                    pe.wait_ge(z_copied, b)
                for r in range(BT):
                    ins = pe.matmul(ps[:, BANK_ACC, r * D:(r + 1) * D], xT[:, r * P:(r + 1) * P], BTs[:, :],
                                    start=True, stop=True)
                ins.then_inc(z_mm, 1)
                for a in range(2):
                    ins = pe.matmul(ps[:, BANK_T + 2 + a, :], w1[:, :], xT[:, a * 512:(a + 1) * 512], start=True, stop=True)
                ins.then_inc(hid_mm, 1)
                pe.wait_ge(hid_made, b + 1)
                if b:
                    pe.wait_ge(r_ready, b)
                for r in range(BT):
                    ins = pe.matmul(ps[:, BANK_OUT, r * D:(r + 1) * D], hid[:, r * P:(r + 1) * P], w2[:, :],
                                    start=True, stop=True)
                ins.then_inc(u_mm, 1)

            for b in range(NBATCH):
                mm_h(NB, 2 * b)
                mm_h(NB, 2 * b + 1)
                turn_h(b)
                if b:
                    mm_z(b - 1)
            mm_z(NBATCH - 1)

            def turn_chunk(m, k, peeled):
                v = T * m + k
                if k % KP == 0:
                    pe.wait_ge(raw2_in[k // KP], 16 * (m + 1))
                if not peeled or k >= TB:
                    pe.wait_ge(lo2_ready, v - TB + 1)
                for r in range(G):
                    ins = pe.transpose(ps[:, BANK_T + k % TB, r * P:(r + 1) * P],
                                       raw2[:, k // KP, r, (k % KP) * P:(k % KP + 1) * P], ident[:, :])
                ins.then_inc(t2_done, 1)

            def mm_az(m, k, peeled):
                pe.wait_ge(lo2_ready, T * m + k + 1)
                if k == 0 and not peeled:
                    pe.wait_ge(acc_copied, m)
                ins = pe.matmul(ps[:, BANK_ACC, :], stat[:, k, :], s_hi[:, k % STAGE, :], start=(k == 0), stop=False)
                if k % KP == KP - 1:
                    ins.then_inc(turned, 1)
                pe.matmul(ps[:, BANK_ACC, :], stat[:, k, :], s_lo[:, k % STAGE, :], start=False,
                          stop=(k == T - 1)).then_inc(p3_done, 1)

            def turn_out(m):
                pe.wait_ge(acc_copied, m)
                for r in range(G):
                    ins = pe.transpose(ps[:, BANK_OUT, r * P:(r + 1) * P], hid[:, r * P:(r + 1) * P], ident[:, :])
                ins.then_inc(o_turned, 1)

            def row_group(m, peeled):
                for k in range(T + LAG):
                    if k < T:
                        turn_chunk(m, k, peeled)
                    if k >= LAG:
                        mm_az(m, k - LAG, peeled)
                    if k == 3 and not peeled:
                        turn_out(m)

            pe.wait_ge(r_ready, NBATCH)
            row_group(0, True)
            with pe.Fori(1, NG) as m:
                row_group(m, False)
            turn_out(NG)


_INS = ["x", "adj", "L0_gnn_W_u", "L0_gnn_diag_u", "L0_gnn_par_u", "L0_gnn_W_i", "L0_gnn_diag_i", "L0_gnn_par_i",
        "L0_gnn_ln_gamma", "L0_gnn_ln_beta", "L1_gnn_t", "L1_gnn_B", "L1_gnn_W1", "L1_gnn_b1", "L1_gnn_W2", "L1_gnn_b2"]


def kernel(**inputs):
    import numpy as _np
    import concourse.bacc as _bacc
    from concourse import mybir as _mybir
    from concourse.bass_utils import run_bass_kernel_spmd as _run

    nc = _bacc.Bacc("TRN2", target_bir_lowering=False, num_devices=1)
    arrays, args = {}, []
    for name in _INS:
        a = _np.ascontiguousarray(inputs[name])
        arrays[f"in_{name}_dram"] = a
        args.append(nc.dram_tensor(f"in_{name}_dram", a.shape, _mybir.dt.from_np(a.dtype), kind="ExternalInput").ap())
    args.append(nc.dram_tensor("out_0_dram", (N, D), F32, kind="ExternalOutput").ap())
    build(nc, *args)
    r = _run(nc, [arrays], core_ids=[0])
    return r.results[0]["out_0_dram"]
```

```python
from contextlib import ExitStack

import concourse.bass as bass
from concourse import mybir

F32 = mybir.dt.float32
F32R = mybir.dt.float32r
ALU = mybir.AluOpType
ACT = mybir.ActivationFunctionType
AX = mybir.AxisListType

P = 128
D = 64
N = 5120
T = N // P
H = 128
USERS = 2048
LN_EPS = 1e-5

W = 256
NB = N // W
CH = W // P
G = 4
NG = T // G
RAW = 5
U = G // 2
NU = T // U
NAT = 5
DOUBLE = 3
P2_AFTER = {2: [0], 3: [1], 4: [2], 5: [3], **{2 * g - 1: [g] for g in range(4, NG)}}
ADD_AFTER = {5: [0], 6: [1], 7: [2], 8: [3], 10: [4], 12: [5], 14: [6], 16: [7], 18: [8], 19: [9]}
MAKE_Y_AFTER = 3

BT = 8
NBATCH = T // BT
ROUNDS = NG + 3

PIECES = 4
PW = N // PIECES
KP = PW // P
STAGE = 5
TB = 4
LAG = 3
FOLD = 832
SUM_AFTER = [1, 3, 6, 8]
EPI_AT = [*range(4, 20, 2), 36]

BANK_YT, BANK_Y = 0, 1
BANK_T = 2
BANK_P2 = 6
BANK_ACC, BANK_OUT = 0, 1
BANK_H = 2
BANK_X1T, BANK_HID, BANK_Z, BANK_U = 4, 5, 0, 1


def build(nc, x, adj, W_u, diag_u, par_u, W_i, diag_i, par_i, ln_gamma, ln_beta, t, B, W1, b1, W2, b2, out):
    ctx = ExitStack()
    with ctx:
        def sb(name, shape, dt=F32, scope=ctx):
            return scope.enter_context(nc.sbuf_tensor(name, shape, dt))

        def sem(name):
            return ctx.enter_context(nc.semaphore(name))

        ps = ctx.enter_context(nc.psum_tensor("ps", [P, 8, 512], F32))

        ident = sb("ident", [P, P])
        ident_r = sb("ident_r", [P, P], F32R)
        X = sb("X", [P, T, D])
        stat = sb("stat", [P, T, 2 * D], F32R)
        hT = sb("hT", [P, N])
        diag = sb("diag", [P, T])
        wu = sb("wu", [D, D])
        wi = sb("wi", [D, D])
        pars = sb("pars", [P, 4])
        pp = sb("pp", [P, 2])
        gam = sb("gam", [P, D])
        bet = sb("bet", [P, D])
        b2r = sb("b2r", [P, D])
        BTs = sb("BTs", [D, D])
        w1 = sb("w1", [D, H])
        w1t = sb("w1t", [P, 1])
        b1c = sb("b1c", [P, 1])
        tc = sb("tc", [P, 1])
        hbias = sb("hbias", [P, 1])
        w2 = sb("w2", [H, D])
        minus_half = sb("minus_half", [P, G])
        add_halves = sb("add_halves", [P, D])
        centre = sb("centre", [P, 2, D])

        hid = sb("hid", [P, G * P])
        dump = hT[:, 0:G * (PW - FOLD)].rearrange("p (r c) -> p r c", r=G)
        accT = sb("accT", [P, G * P])

        with ExitStack() as first:
            AT = sb("AT", [P, NG + DOUBLE, 2, CH, G * P], F32R, first)
            raw = sb("raw", [P, RAW, G, W], scope=first)
            nat_hi = sb("nat_hi", [P, NAT, U, W], F32R, first)
            nat_lo = sb("nat_lo", [P, NAT, U, W], F32R, first)
            yT = sb("yT", [P, W], scope=first)
            ystat = sb("ystat", [P, CH, 2 * D], F32R, first)

        with ExitStack() as before:
            xs = sb("xs", [P, 2, BT, D], scope=before)
            xsT = sb("xsT", [D, 2, BT * P], scope=before)
            ef = sb("ef", [P, 2, BT * D], scope=before)

        with ExitStack() as second:
            raw2 = sb("raw2", [P, PIECES, G, PW], scope=second)
            s_hi = sb("s_hi", [P, STAGE, G * P], F32R, second)
            s_lo = sb("s_lo", [P, STAGE, G * P], F32R, second)
            Z = sb("Z", [P, T, D], scope=second)
            R = sb("R", [P, T, D], scope=second)
            a = sb("a", [P, 2, G, D], scope=second)
            sq1 = sb("sq1", [P, G, D + 1], scope=second)
            sq2 = sb("sq2", [P, G, D + 1], scope=second)
            st = sb("st", [P, 2, 5, G], scope=second)
            x1 = sb("x1", [P, 2, G, D], scope=second)
            xT = sb("xT", [D, G * P], scope=second)
            f1 = sb("f1", [P, G, FOLD // 2], scope=second)
            rsp = sb("rsp", [P, T, 2 * PIECES], scope=second)
            rst = sb("rst", [P, G], scope=second)
            o = sb("o", [P, G, D], scope=second)
            oz = sb("oz", [P, G, D], scope=second)
            osq = sb("osq", [P, G, D + 1], scope=second)
            ost = sb("ost", [P, 3, G], scope=second)

        consts_in = sem("consts_in")
        x_in = sem("x_in")
        raw_in = [sem(f"raw_in{s}") for s in range(RAW)]
        id_zero, id_made, id_round = sem("id_zero"), sem("id_made"), sem("id_round")
        pp_made, hb_made = sem("pp_made"), sem("hb_made")
        xs_made, xs_turned, xsT_copied, e_mm, e_made = (sem(n) for n in ("xs_made", "xs_turned", "xsT_copied", "e_mm", "e_made"))
        e_sum, e_hi = sem("e_sum"), sem("e_hi")
        x_doubled, base_made = sem("x_doubled"), sem("base_made")
        hT_zeroed = sem("hT_zeroed")
        hi_ready = sem("hi_ready")
        lo_dve, lo_pool = sem("lo_dve"), sem("lo_pool")
        t_done, at_ready = sem("t_done"), sem("at_ready")
        p1_done, yT_copied, y_turned = sem("p1_done"), sem("yT_copied"), sem("y_turned")
        y_hi, y_ready = sem("y_hi"), sem("y_ready")
        p2_done, h_added = sem("p2_done"), sem("h_added")
        add_made, centre_made, eps_set = sem("add_made"), sem("centre_made"), sem("eps_set")
        h_centred, sq1_made, sum1_ready, rstd1_ready, h_scaled = (
            sem(n) for n in ("h_centred", "sq1_made", "sum1_ready", "rstd1_ready", "h_scaled"))
        a_ready, a_summed, a_centred, sq2_made, sum2_ready, rstd2_ready, x1_ready = (
            sem(n) for n in ("a_ready", "a_summed", "a_centred", "sq2_made", "sum2_ready", "rstd2_ready", "x1_ready"))
        half_made, orstd_ready = sem("half_made"), sem("orstd_ready")
        x1_turned, xT_copied, z_mm, hid_mm, hid_made, u_mm = (sem(n) for n in ("x1_turned", "xT_copied", "z_mm", "hid_mm", "hid_made", "u_mm"))
        x1b_made, z_copied, z_hi, z_ready, r_ready = (sem(n) for n in ("x1b_made", "z_copied", "z_hi", "z_ready", "r_ready"))
        raw2_in = [sem(f"raw2_in{c}") for c in range(PIECES)]
        t2_done, hi2_ready, lo2_ready, p3_done = sem("t2_done"), sem("hi2_ready"), sem("lo2_ready"), sem("p3_done")
        turned, fold1, fold2, fold3, fold_summed = (sem(n) for n in ("turned", "fold1", "fold2", "fold3", "fold_summed"))
        act_summed = sem("act_summed")
        acc_copied, o_turned, epi_link = sem("acc_copied"), sem("o_turned"), sem("epi_link")
        stored = sem("stored")

        adj_cols = adj.rearrange("(g r p) c -> p g r c", r=G, p=P)
        out_v = out.rearrange("(t p) d -> p t d", p=P)
        x_v = x.rearrange("(t p) d -> p t d", p=P)
        UT = USERS // P
        CONSTS = 15
        RSTD_SCALE = float(D) ** 0.5
        EPI = len(EPI_AT)

        def slot_of(J, g):
            if g >= DOUBLE:
                return g
            return g + NG * (J % 2)

        block = ctx.enter_context(nc.Block())

        @block.sync
        def _(sp):
            sp.dma_start(X[:, :, :], x_v).then_inc(x_in, 16)

            def load_block(J, peeled):
                first_col = J * W if peeled else sp.snap(J * W)
                for g in range(NG):
                    s = g % RAW
                    if not peeled or g >= RAW:
                        done = G // U * (NG * J + g - RAW + 1)
                        sp.wait_ge(lo_dve, done)
                        sp.wait_ge(lo_pool, done)
                    sp.dma_start(raw[:, s, :, :], adj_cols[:, g, :, bass.ds(first_col, W)]).then_inc(raw_in[s], 16)

            load_block(0, True)
            with sp.Fori(1, NB) as J:
                load_block(J, False)

            def load_piece(m, c):
                sp.dma_start(raw2[:, c, :, :], adj_cols[:, m, :, c * PW:(c + 1) * PW]).then_inc(raw2_in[c], 16)

            def store(m):
                first_tile = sp.snap(m * G) if not isinstance(m, int) else m * G
                sp.wait_ge(epi_link, EPI * (m + 1))
                sp.dma_start(out_v[:, bass.ds(first_tile, G), :], R[:, bass.ds(first_tile, G), :]).then_inc(stored, 16)

            for c in range(PIECES):
                last = -(-(c + 1) * G * PW // (2 * CH * G * P)) - 1
                if last < DOUBLE:
                    sp.wait_ge(p2_done, NG * (NB - 2) + last + 1)
                else:
                    sp.wait_ge(p2_done, NG * (NB - 1) + last + 1)
                load_piece(0, c)

            def load_group(m):
                for c in range(PIECES):
                    n = PIECES * (m - 1) + c
                    sp.wait_ge(turned, n + 1)
                    sp.wait_ge(fold1, n + 1)
                    sp.wait_ge(act_summed, n + 1)
                    load_piece(m, c)

            load_group(1)
            with sp.Fori(2, NG) as m:
                load_group(m)
                store(m - 2)
            store(NG - 2)
            store(NG - 1)
            sp.wait_ge(stored, 16 * NG)

        @block.scalar
        def _(act):
            with nc.allow_non_contiguous_dma("small constants, once"):
                for dst, src in (
                    (diag[:, 0:UT], diag_u.rearrange("(t p) -> p t", p=P)),
                    (diag[:, UT:T], diag_i.rearrange("(t p) -> p t", p=P)),
                    (wu[:, :], W_u), (wi[:, :], W_i),
                    (pars[:, 0:2], par_u.partition_broadcast(P)),
                    (pars[:, 2:4], par_i.partition_broadcast(P)),
                    (gam[:, :], ln_gamma.partition_broadcast(P)),
                    (bet[:, :], ln_beta.partition_broadcast(P)),
                    (b2r[:, :], b2.partition_broadcast(P)),
                    (BTs[:, :], B.rearrange("o d -> d o")),
                    (w1[:, :], W1[0:D, :]),
                    (w1t[:, :], W1[D:D + 1, :].rearrange("a h -> h a")),
                    (b1c[:, :], b1.rearrange("(h a) -> h a", a=1)),
                    (tc[:, :], t.partition_broadcast(P)),
                    (w2[:, :], W2),
                ):
                    act.dma_start(dst, src).then_inc(consts_in, 16)

            for b in range(NBATCH):
                act.wait_ge(xs_turned, b + 1)
                if b >= 2:
                    act.wait_ge(e_mm, b - 1)
                act.copy(xsT[:, b % 2, :], ps[0:D, BANK_T + 2:BANK_T + 4, :].rearrange("p a c -> p (a c)")).then_inc(xsT_copied, 1)

            def copy_yT(J):
                act.wait_ge(p1_done, NU * J)
                act.copy(yT[:, :], ps[:, BANK_YT, 0:W]).then_inc(yT_copied, 1)

            def keep_tiles(J, peeled):
                for g in range(NG):
                    for half in range(2):
                        u = 2 * (NG * J + g) + half
                        act.wait_ge(t_done, u + 1)
                        if not peeled and half == 0:
                            if g >= DOUBLE:
                                act.wait_ge(p2_done, NG * (J - 1) + g + 1)
                            else:
                                act.wait_ge(y_turned, J)
                        b0 = BANK_T + 2 * half
                        dst = AT[:, slot_of(J, g), :, :, half * 2 * P:(half + 1) * 2 * P]
                        act.copy(dst.rearrange("p h k (r i) -> p r (h k) i", r=2),
                                 ps[:, b0:b0 + 2, :].rearrange("p r (q i) -> p r q i", i=P)).then_inc(at_ready, 1)

            keep_tiles(0, True)
            with act.Fori(1, NB) as J:
                copy_yT(J)
                keep_tiles(J, False)
            copy_yT(NB)

            for i in range(ROUNDS):
                if 2 <= i < NG + 2:
                    g = i - 2
                    act.wait_ge(x1_turned, g + 1)
                    if g >= 1:
                        act.wait_ge(z_mm, g)
                        act.wait_ge(hid_mm, g)
                    act.copy(xT[:, :], ps[0:D, BANK_X1T, :]).then_inc(xT_copied, 1)
                if 1 <= i < NG + 1:
                    g = i - 1
                    act.wait_ge(a_centred, g + 1)
                    if g >= 1:
                        act.wait_ge(sum2_ready, g)
                    if g == 0:
                        act.wait_ge(eps_set, 3)
                    act.square(sq2[:, :, 0:D], a[:, g % 2, :, :]).then_inc(sq2_made, 1)
                if i < NG:
                    act.wait_ge(h_centred, i + 1)
                    if i >= 1:
                        act.wait_ge(sum1_ready, i)
                    if i == 0:
                        act.wait_ge(eps_set, 3)
                    hv = ps[:, BANK_H + i % 2, :].rearrange("p (t w d) -> p t w d", w=2, d=D)
                    act.square(sq1[:, :, 0:D], hv[:, :, 0, :]).then_inc(sq1_made, 1)
                if 2 <= i < NG + 2:
                    g = i - 2
                    tiles = slice(g * G, (g + 1) * G)
                    zv = ps[:, BANK_Z, 0:G * D].rearrange("p (t d) -> p t d", d=D)
                    act.wait_ge(z_mm, g + 1)
                    act.copy(stat[:, tiles, 0:D], zv).then_inc(z_hi, 1)
                    act.copy(Z[:, tiles, :], zv).then_inc(z_copied, 1)
                    act.wait_ge(hid_mm, g + 1)
                    if g == 0:
                        act.wait_ge(hb_made, 1)
                    else:
                        act.wait_ge(u_mm, g)
                    act.activation(hid[:, :], ps[:, BANK_HID, :], ACT.Tanh, bias=hbias[:, 0:1]).then_inc(hid_made, 1)

            def copy_acc(m):
                act.wait_ge(p3_done, T * m)
                act.copy(accT[:, :], ps[:, BANK_ACC, :]).then_inc(acc_copied, 1)

            def split_hi(m, peeled):
                for k in range(T):
                    v = T * m + k
                    act.wait_ge(t2_done, v + 1)
                    if not peeled or k >= STAGE:
                        act.wait_ge(p3_done, v - STAGE + 1)
                    act.copy(s_hi[:, k % STAGE, :], ps[:, BANK_T + k % TB, :]).then_inc(hi2_ready, 1)
                    if k % KP in SUM_AFTER:
                        c, r = k // KP, SUM_AFTER.index(k % KP)
                        if r == 0:
                            act.wait_ge(raw2_in[c], 16 * (m + 1))
                            if not peeled or c:
                                act.wait_ge(act_summed, PIECES * m + c)
                        ins = act.activation(dump[:, r, :], raw2[:, c, r, FOLD:PW], ACT.Copy,
                                             accum_out=rsp[:, bass.ds(m * G + r, 1), PIECES + c])
                        if r == G - 1:
                            ins.then_inc(act_summed, 1)

            split_hi(0, True)
            with act.Fori(1, NG) as m:
                copy_acc(m)
                split_hi(m, False)
            copy_acc(NG)

        @block.gpsimd
        def _(pool):
            pool.memset(ident[:, :], 0.0).then_inc(id_zero, 1)
            pool.wait_ge(id_zero, 1)
            pool.affine_select(out=ident[:, :], in_=ident[:, :], compare_op=ALU.not_equal, fill=1.0, base=0,
                               pattern=[[-1, P]], channel_multiplier=1).then_inc(id_made, 1)
            pool.wait_ge(id_made, 1)
            pool.tensor_tensor(add_halves[:, :], ident[:, 0:D], ident[:, D:2 * D], ALU.add).then_inc(add_made, 1)
            pool.memset(minus_half[:, :], -0.5).then_inc(half_made, 1)
            pool.memset(hT[:, :], 0.0).then_inc(hT_zeroed, 1)

            def split_lo(J, u):
                half = u % 2
                pool.wait_ge(hi_ready, NU * J + u + 1)
                pool.tensor_tensor(nat_lo[:, u % NAT, 1, :], raw[:, u // 2 % RAW, half * U + 1, :],
                                   nat_hi[:, u % NAT, 1, :].bitcast(F32), ALU.subtract).then_inc(lo_pool, 1)

            pool.wait_ge(consts_in, 16 * CONSTS)
            for u in range(NU):
                split_lo(0, u)
                if u % (NU // NBATCH) == NU // NBATCH - 1:
                    b = u // (NU // NBATCH)
                    xb = X[:, b * BT:(b + 1) * BT, :]
                    pool.wait_ge(e_made, NBATCH)
                    pool.tensor_tensor(xb, xb, xb, ALU.add).then_inc(x_doubled, 1)
                    pool.wait_ge(x_doubled, b + 1)
                    pool.tensor_tensor(xb, xb, bet[:, :].unsqueeze(1).to_broadcast([P, BT, D]), ALU.add).then_inc(base_made, 1)
            with pool.Fori(1, NB) as J:
                for u in range(NU):
                    split_lo(J, u)

            pool.wait_ge(p1_done, NB * NU)
            for squares in (sq1, sq2, osq):
                pool.memset(squares[:, :, D], LN_EPS * D).then_inc(eps_set, 1)

            def rstd(of, i, ready):
                pool.tensor_tensor(st[:, i % 2, of + 1, :], st[:, i % 2, of, :], minus_half[:, :], ALU.pow).then_inc(ready, 1)

            for i in range(NG + 1):
                if i < NG:
                    pool.wait_ge(sum1_ready, i + 1)
                    if i >= 2:
                        pool.wait_ge(h_scaled, i - 1)
                    rstd(0, i, rstd1_ready)
                if i >= 1:
                    pool.wait_ge(sum2_ready, i)
                    if i >= 3:
                        pool.wait_ge(x1_ready, i - 2)
                    rstd(2, i - 1, rstd2_ready)
                if i < NG:
                    pool.wait_ge(h_scaled, i + 1)
                    pool.tensor_tensor(a[:, i % 2, :, :], a[:, i % 2, :, :], X[:, i * G:(i + 1) * G, :], ALU.add).then_inc(a_ready, 1)
                if i >= 1:
                    pool.wait_ge(x1_ready, i)
                    pool.tensor_tensor(R[:, (i - 1) * G:i * G, :], x1[:, (i - 1) % 2, :, :],
                                       b2r[:, :].unsqueeze(1).to_broadcast([P, G, D]), ALU.add).then_inc(x1b_made, 1)

            def rstd_of_out(m):
                pool.wait_ge(epi_link, EPI * m + EPI - 1)
                pool.tensor_tensor(ost[:, 2, :], ost[:, 1, :], minus_half[:, 0:G], ALU.pow).then_inc(orstd_ready, 1)

            def fold(m, peeled):
                for c in range(PIECES):
                    if not peeled and c == 2:
                        rstd_of_out(m - 1)
                    n = PIECES * m + c
                    q = FOLD // 2
                    pool.wait_ge(raw2_in[c], 16 * (m + 1))
                    if not peeled or c:
                        pool.wait_ge(fold_summed, n)
                    pool.tensor_tensor(f1[:, :, :], raw2[:, c, :, 0:q], raw2[:, c, :, q:2 * q], ALU.add).then_inc(fold1, 1)
                    pool.wait_ge(fold1, n + 1)
                    q //= 2
                    pool.tensor_tensor(f1[:, :, 0:q], f1[:, :, 0:q], f1[:, :, q:2 * q], ALU.add).then_inc(fold2, 1)
                    pool.wait_ge(fold2, n + 1)
                    q //= 2
                    pool.tensor_tensor(f1[:, :, 0:q], f1[:, :, 0:q], f1[:, :, q:2 * q], ALU.add).then_inc(fold3, 1)

            fold(0, True)
            with pool.Fori(1, NG) as m:
                fold(m, False)
            rstd_of_out(NG - 1)

        @block.vector
        def _(dve):
            dve.wait_ge(id_made, 1)
            dve.tensor_copy(ident_r[:, :], ident[:, :]).then_inc(id_round, 1)
            dve.wait_ge(consts_in, 16 * CONSTS)
            dve.tensor_tensor(pp[:, :], pars[:, 0:4:2], pars[:, 1:4:2], ALU.mult).then_inc(pp_made, 1)
            dve.scalar_tensor_tensor(hbias[:, :], w1t[:, :], tc[:, 0:1], b1c[:, :], ALU.mult, ALU.add).then_inc(hb_made, 1)
            dve.wait_ge(add_made, 1)
            dve.tensor_scalar(centre[:, 0, :], add_halves[:, :], -1.0 / D, None, ALU.add).then_inc(centre_made, 1)
            dve.wait_ge(centre_made, 1)
            dve.tensor_tensor(centre[:, 1, :], centre[:, 0, :], gam[:, :], ALU.mult).then_inc(centre_made, 1)
            dve.wait_ge(x_in, 16)

            def scale_x(b):
                if b >= 2:
                    dve.wait_ge(xs_turned, b - 1)
                dve.tensor_tensor(xs[:, b % 2, :, :], X[:, b * BT:(b + 1) * BT, :],
                                  diag[:, b * BT:(b + 1) * BT].unsqueeze(2).to_broadcast([P, BT, D]),
                                  ALU.mult).then_inc(xs_made, 1)

            def make_e(b):
                who = 0 if b * BT < UT else 1
                dve.wait_ge(e_mm, b + 1)
                if b == 0:
                    dve.wait_ge(pp_made, 1)
                e = ef[:, b % 2, :]
                dve.scalar_tensor_tensor(e, ps[:, BANK_P2 + b % 2, :], pp[:, who:who + 1],
                                         X[:, b * BT:(b + 1) * BT, :].rearrange("p t d -> p (t d)"),
                                         ALU.mult, ALU.add).then_inc(e_sum, 1)
                dve.wait_ge(e_sum, b + 1)
                dst = stat[:, b * BT:(b + 1) * BT, :]
                ev = e.rearrange("p (t d) -> p t d", d=D)
                dve.tensor_copy(dst[:, :, 0:D], ev).then_inc(e_hi, 1)
                dve.wait_ge(e_hi, b + 1)
                dve.tensor_tensor(dst[:, :, D:2 * D], ev, dst[:, :, 0:D].bitcast(F32), ALU.subtract).then_inc(e_made, 1)

            scale_x(0)
            scale_x(1)
            for b in range(NBATCH):
                make_e(b)
                if b + 2 < NBATCH:
                    scale_x(b + 2)

            def split(J, u, peeled):
                n = NU * J + u
                g, half = u // 2, u % 2
                s = g % RAW
                if half == 0:
                    dve.wait_ge(raw_in[s], 16 * (NG // RAW * J + g // RAW + 1))
                if not peeled or u >= NAT:
                    dve.wait_ge(p1_done, n - NAT + 1)
                dve.tensor_copy(nat_hi[:, u % NAT, :, :], raw[:, s, half * U:(half + 1) * U, :]).then_inc(hi_ready, 1)
                dve.wait_ge(hi_ready, n + 1)
                dve.tensor_tensor(nat_lo[:, u % NAT, 0, :], raw[:, s, half * U, :], nat_hi[:, u % NAT, 0, :].bitcast(F32),
                                  ALU.subtract).then_inc(lo_dve, 1)

            def make_y(J):
                dve.wait_ge(y_turned, J)
                yv = ps[:, BANK_Y, 0:CH * D].rearrange("p (k d) -> p k d", d=D)
                dve.tensor_copy(ystat[:, :, 0:D], yv).then_inc(y_hi, 1)
                dve.wait_ge(y_hi, J)
                dve.tensor_tensor(ystat[:, :, D:2 * D], yv, ystat[:, :, 0:D].bitcast(F32), ALU.subtract).then_inc(y_ready, 1)

            def add_h(J, g):
                dve.wait_ge(p2_done, NG * (J - 1) + g + 1)
                cols = hT[:, g * G * P:(g + 1) * G * P]
                dve.tensor_tensor(cols, cols, ps[:, BANK_P2 + g % 2, :], ALU.add).then_inc(h_added, 1)

            for u in range(NU):
                split(0, u, True)
            dve.wait_ge(hT_zeroed, 1)
            with dve.Fori(1, NB) as J:
                for u in range(NU):
                    split(J, u, False)
                    if u == MAKE_Y_AFTER:
                        make_y(J)
                    for g in ADD_AFTER.get(u, []):
                        add_h(J, g)
            make_y(NB)

            def inner_sum(dst, src):
                return dve.tensor_reduce(dst, src, AX.X, ALU.add)

            wide = [P, G, D]

            for i in range(ROUNDS):
                if i < NG:
                    add_h(NB, i)
                if 1 <= i < NG + 1:
                    g = i - 1
                    ag, sg = a[:, g % 2, :, :], st[:, g % 2, :, :]
                    dve.wait_ge(a_ready, g + 1)
                    inner_sum(sg[:, 4, :], ag).then_inc(a_summed, 1)
                    dve.wait_ge(a_summed, g + 1)
                    dve.scalar_tensor_tensor(ag, sg[:, 4, :].unsqueeze(2).to_broadcast(wide), 1.0 / D, ag,
                                             ALU.mult, ALU.subtract).then_inc(a_centred, 1)
                if i >= 3:
                    g = i - 3
                    dve.wait_ge(u_mm, g + 1)
                    dve.wait_ge(x1b_made, g + 1)
                    rg = R[:, g * G:(g + 1) * G, :]
                    dve.tensor_tensor(rg, rg, ps[:, BANK_U, 0:G * D].rearrange("p (t d) -> p t d", d=D),
                                      ALU.add).then_inc(r_ready, 1)
                if i < NG:
                    dve.wait_ge(sq1_made, i + 1)
                    inner_sum(st[:, i % 2, 0, :], sq1[:, :, :]).then_inc(sum1_ready, 1)
                if 1 <= i < NG + 1:
                    g = i - 1
                    dve.wait_ge(sq2_made, g + 1)
                    inner_sum(st[:, g % 2, 2, :], sq2[:, :, :]).then_inc(sum2_ready, 1)
                if i < NG:
                    dve.wait_ge(rstd1_ready, i + 1)
                    hv = ps[:, BANK_H + i % 2, :].rearrange("p (t w d) -> p t w d", w=2, d=D)
                    if i >= 2:
                        dve.wait_ge(x1_ready, i - 1)
                    dve.scalar_tensor_tensor(a[:, i % 2, :, :], hv[:, :, 1, :], RSTD_SCALE,
                                             st[:, i % 2, 1, :].unsqueeze(2).to_broadcast(wide),
                                             ALU.mult, ALU.mult).then_inc(h_scaled, 1)
                if 1 <= i < NG + 1:
                    g = i - 1
                    dve.wait_ge(rstd2_ready, g + 1)
                    if g >= 2:
                        dve.wait_ge(x1b_made, g - 1)
                        dve.wait_ge(x1_turned, g - 1)
                    dve.scalar_tensor_tensor(x1[:, g % 2, :, :], a[:, g % 2, :, :], -RSTD_SCALE,
                                             st[:, g % 2, 3, :].unsqueeze(2).to_broadcast(wide),
                                             ALU.mult, ALU.mult).then_inc(x1_ready, 1)
                if 2 <= i < NG + 2:
                    g = i - 2
                    tiles = slice(g * G, (g + 1) * G)
                    dve.wait_ge(z_copied, g + 1)
                    dve.tensor_tensor(stat[:, tiles, D:2 * D], ps[:, BANK_Z, 0:G * D].rearrange("p (t d) -> p t d", d=D),
                                      stat[:, tiles, 0:D].bitcast(F32), ALU.subtract).then_inc(z_ready, 1)

            def epilogue(m, s):
                if s:
                    dve.wait_ge(epi_link, EPI * m + s)
                rows = bass.ds(m * G, G)
                if s == 0:
                    dve.wait_ge(fold_summed, PIECES * (m + 1))
                    dve.wait_ge(act_summed, PIECES * (m + 1))
                    ins = inner_sum(rst[:, :], rsp[:, rows, :])
                elif s == 1:
                    ins = dve.tensor_tensor(oz[:, :, :], Z[:, rows, :], rst[:, :].unsqueeze(2).to_broadcast(wide), ALU.mult)
                elif s == 2:
                    ins = dve.tensor_tensor(o[:, :, :], R[:, rows, :], oz[:, :, :], ALU.subtract)
                elif s == 3:
                    dve.wait_ge(o_turned, m + 1)
                    ins = dve.tensor_tensor(o[:, :, :], o[:, :, :],
                                            ps[:, BANK_OUT, 0:G * D].rearrange("p (r d) -> p r d", d=D), ALU.add)
                elif s == 4:
                    ins = inner_sum(ost[:, 0, :], o[:, :, :])
                elif s == 5:
                    ins = dve.scalar_tensor_tensor(o[:, :, :], ost[:, 0, :].unsqueeze(2).to_broadcast(wide), 1.0 / D,
                                                   o[:, :, :], ALU.mult, ALU.subtract)
                elif s == 6:
                    ins = dve.tensor_tensor(osq[:, :, 0:D], o[:, :, :], o[:, :, :], ALU.mult)
                elif s == 7:
                    ins = inner_sum(ost[:, 1, :], osq[:, :, :])
                else:
                    dve.wait_ge(orstd_ready, m + 1)
                    ins = dve.scalar_tensor_tensor(R[:, rows, :], o[:, :, :], -RSTD_SCALE,
                                                   ost[:, 2, :].unsqueeze(2).to_broadcast(wide), ALU.mult, ALU.mult)
                ins.then_inc(epi_link, 1)

            def split_lo(m, peeled):
                for k in range(T):
                    v = T * m + k
                    dve.wait_ge(hi2_ready, v + 1)
                    dve.tensor_tensor(s_lo[:, k % STAGE, :], ps[:, BANK_T + k % TB, :],
                                      s_hi[:, k % STAGE, :].bitcast(F32), ALU.subtract).then_inc(lo2_ready, 1)
                    if not peeled and k in EPI_AT:
                        epilogue(m - 1, EPI_AT.index(k))
                    if k % KP == KP - 1:
                        c = k // KP
                        dve.wait_ge(fold3, PIECES * m + c + 1)
                        inner_sum(rsp[:, bass.ds(m * G, G), c], f1[:, :, 0:FOLD // 8]).then_inc(fold_summed, 1)

            split_lo(0, True)
            with dve.Fori(1, NG) as m:
                split_lo(m, False)
            for s in range(EPI):
                epilogue(NG - 1, s)

        @block.tensor
        def _(pe):
            pe.wait_ge(id_made, 1)
            pe.wait_ge(consts_in, 16 * CONSTS)

            def turn_xs(b):
                pe.wait_ge(xs_made, b + 1)
                if b:
                    pe.wait_ge(xsT_copied, b)
                for r in range(BT):
                    ins = pe.transpose(ps[0:D, BANK_T + 2 + r // 4, (r % 4) * P:(r % 4 + 1) * P], xs[:, b % 2, r, :], ident[:, :])
                ins.then_inc(xs_turned, 1)

            def mm_e(b):
                pe.wait_ge(xsT_copied, b + 1)
                if b >= 2:
                    pe.wait_ge(e_sum, b - 1)
                w = wu if b * BT < UT else wi
                for r in range(BT):
                    ins = pe.matmul(ps[:, BANK_P2 + b % 2, r * D:(r + 1) * D], xsT[:, b % 2, r * P:(r + 1) * P], w[:, :],
                                    start=True, stop=True)
                ins.then_inc(e_mm, 1)

            turn_xs(0)
            for b in range(NBATCH):
                if b + 1 < NBATCH:
                    turn_xs(b + 1)
                mm_e(b)

            def turn_tiles(J, u, peeled):
                n = NU * J + u
                pe.wait_ge(lo_dve, n + 1)
                pe.wait_ge(lo_pool, n + 1)
                if not peeled or u >= 2:
                    pe.wait_ge(at_ready, n - 1)
                for r in range(U):
                    for h, part in enumerate((nat_hi, nat_lo)):
                        for k in range(CH):
                            q = h * CH + k
                            ins = pe.transpose(ps[:, BANK_T + u % 2 * U + r, q * P:(q + 1) * P].bitcast(F32R),
                                               part[:, u % NAT, r, k * P:(k + 1) * P], ident_r[:, :])
                ins.then_inc(t_done, 1)

            def mm_y(u):
                for r in range(U):
                    i = u * U + r
                    for part in (nat_hi, nat_lo):
                        ins = pe.matmul(ps[:, BANK_YT, 0:W], stat[:, i, :], part[:, u % NAT, r, :],
                                        start=(i == 0 and part is nat_hi), stop=(i == T - 1 and part is nat_lo))
                ins.then_inc(p1_done, 1)

            def turn_y(J):
                pe.wait_ge(yT_copied, J)
                for k in range(CH):
                    ins = pe.matmul(ps[:, BANK_Y, k * D:(k + 1) * D], yT[:, k * P:(k + 1) * P], add_halves[:, :],
                                    start=True, stop=True)
                ins.then_inc(y_turned, 1)

            def mm_h(J, g):
                if g == 0:
                    pe.wait_ge(y_ready, J)
                pe.wait_ge(at_ready, 2 * (NG * (J - 1) + g + 1))
                if g >= 2:
                    pe.wait_ge(h_added, NG * (J - 1) + g - 1)
                for k in range(CH):
                    for h in range(2):
                        ins = pe.matmul(ps[:, BANK_P2 + g % 2, :], ystat[:, k, :], AT[:, slot_of(J - 1, g), h, k, :],
                                        start=(k == 0 and h == 0), stop=(k == CH - 1 and h == 1))
                ins.then_inc(p2_done, 1)

            def block_products(J, peeled):
                turn_tiles(J, 0, peeled)
                for u in range(NU):
                    if u == 0 and not peeled:
                        turn_tiles(J, 1, peeled)
                        turn_y(J)
                    elif u != 1 and u or peeled and u:
                        turn_tiles(J, u, peeled)
                    mm_y(u)
                    if not peeled:
                        for g in P2_AFTER.get(u, []):
                            mm_h(J, g)

            pe.wait_ge(id_round, 1)
            pe.wait_ge(centre_made, 2)
            pe.wait_ge(e_made, NBATCH)
            block_products(0, True)
            with pe.Fori(1, NB) as J:
                block_products(J, False)
            turn_y(NB)

            def centre_h(g):
                pe.wait_ge(h_added, NG * (NB - 1) + g + 1)
                if g >= 2:
                    pe.wait_ge(h_scaled, g - 1)
                elif g == 0:
                    pe.wait_ge(at_ready, NB * NU)
                for r in range(G):
                    i = g * G + r
                    ins = pe.matmul(ps[:, BANK_H + g % 2, r * P:(r + 1) * P], hT[:, i * P:(i + 1) * P],
                                    centre[:, :, :].rearrange("p w d -> p (w d)"), start=True, stop=True)
                ins.then_inc(h_centred, 1)

            def turn_x1(g):
                pe.wait_ge(x1_ready, g + 1)
                if g:
                    pe.wait_ge(xT_copied, g)
                for r in range(G):
                    ins = pe.transpose(ps[0:D, BANK_X1T, r * P:(r + 1) * P], x1[:, g % 2, r, :], ident[:, :])
                ins.then_inc(x1_turned, 1)

            def mm_z(g):
                pe.wait_ge(xT_copied, g + 1)
                if g:
                    pe.wait_ge(z_copied, g)
                    pe.wait_ge(z_ready, g)
                for r in range(G):
                    ins = pe.matmul(ps[:, BANK_Z, r * D:(r + 1) * D], xT[:, r * P:(r + 1) * P], BTs[:, :],
                                    start=True, stop=True)
                ins.then_inc(z_mm, 1)
                if g:
                    pe.wait_ge(hid_made, g)
                pe.matmul(ps[:, BANK_HID, :], w1[:, :], xT[:, :], start=True, stop=True).then_inc(hid_mm, 1)

            def mm_u(g):
                pe.wait_ge(hid_made, g + 1)
                if g:
                    pe.wait_ge(r_ready, g)
                for r in range(G):
                    ins = pe.matmul(ps[:, BANK_U, r * D:(r + 1) * D], hid[:, r * P:(r + 1) * P], w2[:, :],
                                    start=True, stop=True)
                ins.then_inc(u_mm, 1)

            for i in range(ROUNDS):
                if i < NG:
                    mm_h(NB, i)
                if 2 <= i < NG + 2:
                    turn_x1(i - 2)
                if i >= 3:
                    mm_u(i - 3)
                if i < NG:
                    centre_h(i)
                if 2 <= i < NG + 2:
                    mm_z(i - 2)

            def turn_chunk(m, k, peeled):
                v = T * m + k
                if k % KP == 0:
                    pe.wait_ge(raw2_in[k // KP], 16 * (m + 1))
                if not peeled or k >= TB:
                    pe.wait_ge(lo2_ready, v - TB + 1)
                for r in range(G):
                    ins = pe.transpose(ps[:, BANK_T + k % TB, r * P:(r + 1) * P],
                                       raw2[:, k // KP, r, (k % KP) * P:(k % KP + 1) * P], ident[:, :])
                ins.then_inc(t2_done, 1)

            def mm_az(m, k, peeled):
                pe.wait_ge(lo2_ready, T * m + k + 1)
                if k == 0 and not peeled:
                    pe.wait_ge(acc_copied, m)
                ins = pe.matmul(ps[:, BANK_ACC, :], stat[:, k, :], s_hi[:, k % STAGE, :], start=(k == 0), stop=False)
                if k % KP == KP - 1:
                    ins.then_inc(turned, 1)
                pe.matmul(ps[:, BANK_ACC, :], stat[:, k, :], s_lo[:, k % STAGE, :], start=False,
                          stop=(k == T - 1)).then_inc(p3_done, 1)

            def turn_out(m):
                pe.wait_ge(acc_copied, m)
                for r in range(G):
                    ins = pe.matmul(ps[:, BANK_OUT, r * D:(r + 1) * D], accT[:, r * P:(r + 1) * P], add_halves[:, :],
                                    start=True, stop=True)
                ins.then_inc(o_turned, 1)

            def row_group(m, peeled):
                for k in range(T + LAG):
                    if k < T:
                        turn_chunk(m, k, peeled)
                    if k >= LAG:
                        mm_az(m, k - LAG, peeled)
                    if k == 3 and not peeled:
                        turn_out(m)

            pe.wait_ge(hid_made, NG)
            pe.wait_ge(z_ready, NG)
            pe.wait_ge(z_copied, NG)
            pe.wait_ge(r_ready, NG)
            row_group(0, True)
            with pe.Fori(1, NG) as m:
                row_group(m, False)
            turn_out(NG)


_INS = ["x", "adj", "L0_gnn_W_u", "L0_gnn_diag_u", "L0_gnn_par_u", "L0_gnn_W_i", "L0_gnn_diag_i", "L0_gnn_par_i",
        "L0_gnn_ln_gamma", "L0_gnn_ln_beta", "L1_gnn_t", "L1_gnn_B", "L1_gnn_W1", "L1_gnn_b1", "L1_gnn_W2", "L1_gnn_b2"]


def kernel(**inputs):
    import numpy as _np
    import concourse.bacc as _bacc
    from concourse import mybir as _mybir
    from concourse.bass_utils import run_bass_kernel_spmd as _run

    nc = _bacc.Bacc("TRN2", target_bir_lowering=False, num_devices=1)
    arrays, args = {}, []
    for name in _INS:
        a = _np.ascontiguousarray(inputs[name])
        arrays[f"in_{name}_dram"] = a
        args.append(nc.dram_tensor(f"in_{name}_dram", a.shape, _mybir.dt.from_np(a.dtype), kind="ExternalInput").ap())
    args.append(nc.dram_tensor("out_0_dram", (N, D), F32, kind="ExternalOutput").ap())
    build(nc, *args)
    r = _run(nc, [arrays], core_ids=[0])
    return r.results[0]["out_0_dram"]
```

```python
from contextlib import ExitStack

import concourse.bass as bass
from concourse import mybir

F32 = mybir.dt.float32
F32R = mybir.dt.float32r
ALU = mybir.AluOpType
ACT = mybir.ActivationFunctionType
AX = mybir.AxisListType

P = 128
D = 64
N = 5120
T = N // P
H = 128
USERS = 2048
LN_EPS = 1e-5

W = 256
NB = N // W
CH = W // P
G = 4
NG = T // G
RAW = 5
U = G // 2
NU = T // U
NAT = 5
DOUBLE = [NG - 1, NG - 2, 0]
P2_AFTER = {1: [0, 1], **{2 * g - 1: [g] for g in range(2, NG - 2)}, NU - 3: [NG - 2], NU - 1: [NG - 1]}
ADD_AFTER = {4: [0], 5: [1], **{2 * g + 3: [g] for g in range(2, NG - 2)}}
ADD_LATE_AFTER = {1: [NG - 2], 3: [NG - 1]}
ALONE = [NG - 2]
MAKE_Y_AFTER = 3

X_PARTS = [G, 3 * G, 6 * G, T]
ROUNDS = NG + 4

PIECES = 4
PW = N // PIECES
KP = PW // P
STAGE = 5
TB = 4
LAG = 3
FOLD = 832
SUM_AFTER = [1, 3, 6, 8]
EPI_AT = [4, 5, 6, *range(8, 20, 2), 36]

BANK_YT, BANK_Y = 0, 1
BANK_T = 2
BANK_P2 = 6
BANK_XST, BANK_E = 6, 7
BANK_H = 2
BANK_X1T, BANK_HID, BANK_Z, BANK_U = 4, 5, 0, 1
BANK_ACC = 6
BANK_OUT = 1


def build(nc, x, adj, W_u, diag_u, par_u, W_i, diag_i, par_i, ln_gamma, ln_beta, t, B, W1, b1, W2, b2, out):
    ctx = ExitStack()
    with ctx:
        def sb(name, shape, dt=F32, scope=ctx):
            return scope.enter_context(nc.sbuf_tensor(name, shape, dt))

        def sem(name):
            return ctx.enter_context(nc.semaphore(name))

        ps = ctx.enter_context(nc.psum_tensor("ps", [P, 8, 512], F32))

        ident = sb("ident", [P, P])
        ident_r = sb("ident_r", [P, P], F32R)
        X = sb("X", [P, T, D])
        stat = sb("stat", [P, T, 2 * D], F32R)
        hT = sb("hT", [P, N])
        diag = sb("diag", [P, T])
        wu = sb("wu", [D, D])
        wi = sb("wi", [D, D])
        pars = sb("pars", [P, 4])
        pp = sb("pp", [P, 2])
        gam = sb("gam", [P, D])
        bet = sb("bet", [P, D])
        b2r = sb("b2r", [P, D])
        diag_rows = sb("diag_rows", [T, P])
        Bs = sb("Bs", [D, D])
        BTs = sb("BTs", [D, D])
        w1 = sb("w1", [D, H])
        w1t = sb("w1t", [P, 1])
        b1c = sb("b1c", [P, 1])
        tc = sb("tc", [P, 1])
        hbias = sb("hbias", [P, 1])
        w2 = sb("w2", [H, D])
        minus_half = sb("minus_half", [P, G])
        add_halves = sb("add_halves", [P, D])
        centre = sb("centre", [P, 2, D])

        hid = sb("hid", [P, G * P])
        dump = hT[:, 0:G * (PW - FOLD)].rearrange("p (r c) -> p r c", r=G)
        accT = sb("accT", [P, G * P])

        with ExitStack() as first:
            AT = sb("AT", [P, NG + len(DOUBLE), 2, CH, G * P], F32R, first)
            raw = sb("raw", [P, RAW, G, W], scope=first)
            nat_hi = sb("nat_hi", [P, NAT, U, W], F32R, first)
            nat_lo = sb("nat_lo", [P, NAT, U, W], F32R, first)
            yT = sb("yT", [P, W], scope=first)
            ystat = sb("ystat", [P, CH, 2 * D], F32R, first)

        xs = hT[:, 0:2 * G * D].rearrange("p (s t d) -> p s t d", s=2, d=D)
        ef = hT[:, 2 * G * D:3 * G * D]
        xsT = hT[0:D, 3 * G * D:3 * G * D + G * P]

        SCRATCH = 3 * G * D + G * P

        with ExitStack() as second:
            raw2 = sb("raw2", [P, PIECES, G, PW], scope=second)
            s_hi = sb("s_hi", [P, STAGE, G * P], F32R, second)
            s_lo = sb("s_lo", [P, STAGE, G * P], F32R, second)
            Z = sb("Z", [P, T, D], scope=second)
            R = sb("R", [P, T, D], scope=second)
            a = sb("a", [P, 2, G, D], scope=second)
            sq = sb("sq", [P, 2, G, D + 1], scope=second)
            sums = sb("sums", [P, G], scope=second)
            sqsum = sb("sqsum", [P, 2, G], scope=second)
            rstd = sb("rstd", [P, 2, G], scope=second)
            x1 = sb("x1", [P, 2, G, D], scope=second)
            xT = sb("xT", [D, G * P], scope=second)
            f1 = sb("f1", [P, G, FOLD // 2], scope=second)
            rsp = sb("rsp", [P, T, 2 * PIECES], scope=second)
            rst = sb("rst", [P, G], scope=second)
            o = sb("o", [P, G, D], scope=second)
            oz = sb("oz", [P, G, D], scope=second)
            osq = sb("osq", [P, G, D + 1], scope=second)
            ost = sb("ost", [P, 3, G], scope=second)

        e_consts_in, consts_in = sem("e_consts_in"), sem("consts_in")
        x_in = [sem(f"x_in{i}") for i in range(len(X_PARTS))]
        diag_turned, diag_made, B_turned, BT_made = sem("diag_turned"), sem("diag_made"), sem("B_turned"), sem("BT_made")
        raw_in = [sem(f"raw_in{s}") for s in range(RAW)]
        id_zero, id_made, id_round = sem("id_zero"), sem("id_made"), sem("id_round")
        pp_made, hb_made = sem("pp_made"), sem("hb_made")
        xs_made, xs_turned, xsT_copied, e_mm, e_made = (sem(n) for n in ("xs_made", "xs_turned", "xsT_copied", "e_mm", "e_made"))
        e_sum, e_hi = sem("e_sum"), sem("e_hi")
        x_doubled, base_made = sem("x_doubled"), sem("base_made")
        hT_zeroed, scratch_zeroed = sem("hT_zeroed"), sem("scratch_zeroed")
        hi_ready = sem("hi_ready")
        lo_dve, lo_pool = sem("lo_dve"), sem("lo_pool")
        t_done, at_ready = sem("t_done"), sem("at_ready")
        p1_done, yT_copied, y_turned = sem("p1_done"), sem("yT_copied"), sem("y_turned")
        y_hi, y_ready = sem("y_hi"), sem("y_ready")
        p2_done, h_added = sem("p2_done"), sem("h_added")
        add_made, centre_made, eps_set = sem("add_made"), sem("centre_made"), sem("eps_set")
        h_centred, sq1_made, sq1_summed, rstd1_ready, h_scaled = (
            sem(n) for n in ("h_centred", "sq1_made", "sq1_summed", "rstd1_ready", "h_scaled"))
        sq2_made, sq2_summed, rstd2_ready = sem("sq2_made"), sem("sq2_summed"), sem("rstd2_ready")
        a_ready, a_summed, a_centred, x1_ready = (sem(n) for n in ("a_ready", "a_summed", "a_centred", "x1_ready"))
        half_made, orstd_ready = sem("half_made"), sem("orstd_ready")
        x1_turned, xT_copied, z_mm, hid_mm, hid_made, u_mm = (
            sem(n) for n in ("x1_turned", "xT_copied", "z_mm", "hid_mm", "hid_made", "u_mm"))
        x1b_made, z_copied, z_hi, z_ready, r_ready = (sem(n) for n in ("x1b_made", "z_copied", "z_hi", "z_ready", "r_ready"))
        raw2_in = [sem(f"raw2_in{c}") for c in range(PIECES)]
        t2_done, hi2_ready, lo2_ready, p3_done = sem("t2_done"), sem("hi2_ready"), sem("lo2_ready"), sem("p3_done")
        turned, fold1, fold2, fold3, fold_summed = (sem(n) for n in ("turned", "fold1", "fold2", "fold3", "fold_summed"))
        act_summed = sem("act_summed")
        acc_copied, o_turned, epi_link = sem("acc_copied"), sem("o_turned"), sem("epi_link")
        stored = sem("stored")

        adj_cols = adj.rearrange("(g r p) c -> p g r c", r=G, p=P)
        out_v = out.rearrange("(t p) d -> p t d", p=P)
        x_v = x.rearrange("(t p) d -> p t d", p=P)
        UT = USERS // P
        E_CONSTS, CONSTS = 7, 8
        RSTD_SCALE = float(D) ** 0.5
        EPI = len(EPI_AT)

        def slot_of(J, g):
            if g in DOUBLE:
                return g + (NG + DOUBLE.index(g) - g) * (J % 2)
            return g

        def acc(m):
            if isinstance(m, int):
                return ps[:, BANK_ACC + m % 2, :]
            return ps[:, bass.ds(m % 2 + BANK_ACC, 1), :].rearrange("p a c -> p (a c)")

        block = ctx.enter_context(nc.Block())

        @block.sync
        def _(sp):
            def load_x(i):
                tiles = slice(X_PARTS[i - 1] if i else 0, X_PARTS[i])
                sp.dma_start(X[:, tiles, :], x_v[:, tiles, :]).then_inc(x_in[i], 16)

            def load_consts():
                with nc.allow_non_contiguous_dma("small constants, once"):
                    for dst, src in (
                        (gam[:, :], ln_gamma.partition_broadcast(P)),
                        (b2r[:, :], b2.partition_broadcast(P)),
                        (Bs[:, :], B),
                        (w1[:, :], W1[0:D, :]),
                        (w1t[:, :], W1[D:D + 1, :].rearrange("a h -> h a")),
                        (b1c[:, :], b1.rearrange("(h a) -> h a", a=1)),
                        (tc[:, :], t.partition_broadcast(P)),
                        (w2[:, :], W2),
                    ):
                        sp.dma_start(dst, src).then_inc(consts_in, 16)

            def load_block(J, peeled):
                first_col = J * W if peeled else sp.snap(J * W)
                for g in range(NG):
                    if peeled and 1 <= g < len(X_PARTS):
                        load_x(g)
                    if peeled and g == RAW:
                        load_consts()
                    s = g % RAW
                    if not peeled or g >= RAW:
                        done = G // U * (NG * J + g - RAW + 1)
                        sp.wait_ge(lo_dve, done)
                        sp.wait_ge(lo_pool, done)
                    sp.dma_start(raw[:, s, :, :], adj_cols[:, g, :, bass.ds(first_col, W)]).then_inc(raw_in[s], 16)

            load_x(0)
            with nc.allow_non_contiguous_dma("small constants, once"):
                sp.dma_start(wu[:, :], W_u).then_inc(e_consts_in, 16)
                sp.dma_start(wi[:, :], W_i).then_inc(e_consts_in, 16)
                sp.dma_start(pars[:, 0:2], par_u.partition_broadcast(P)).then_inc(e_consts_in, 16)
            load_block(0, True)
            with sp.Fori(1, NB) as J:
                load_block(J, False)

            def load_piece(m, c):
                sp.dma_start(raw2[:, c, :, :], adj_cols[:, m, :, c * PW:(c + 1) * PW]).then_inc(raw2_in[c], 16)

            def store(m):
                first_tile = sp.snap(m * G) if not isinstance(m, int) else m * G
                sp.wait_ge(epi_link, EPI * (m + 1))
                sp.dma_start(out_v[:, bass.ds(first_tile, G), :], R[:, bass.ds(first_tile, G), :]).then_inc(stored, 16)

            for c in range(PIECES):
                last = -(-(c + 1) * G * PW // (2 * CH * G * P)) - 1
                sp.wait_ge(p2_done, NG * (NB - 1) + last + 1)
                load_piece(0, c)

            def load_group(m):
                for c in range(PIECES):
                    n = PIECES * (m - 1) + c
                    sp.wait_ge(turned, n + 1)
                    sp.wait_ge(fold1, n + 1)
                    sp.wait_ge(act_summed, n + 1)
                    load_piece(m, c)

            load_group(1)
            with sp.Fori(2, NG) as m:
                load_group(m)
                store(m - 2)
            store(NG - 2)
            store(NG - 1)
            sp.wait_ge(stored, 16 * NG)

        @block.scalar
        def _(act):
            with nc.allow_non_contiguous_dma("small constants, once"):
                for dst, src in (
                    (diag_rows[0:UT, :], diag_u.rearrange("(t p) -> t p", p=P)),
                    (diag_rows[UT:T, :], diag_i.rearrange("(t p) -> t p", p=P)),
                    (pars[:, 2:4], par_i.partition_broadcast(P)),
                    (bet[:, :], ln_beta.partition_broadcast(P)),
                ):
                    act.dma_start(dst, src).then_inc(e_consts_in, 16)

            def copy_xsT(g):
                act.wait_ge(xs_turned, g + 1)
                if g:
                    act.wait_ge(e_mm, g)
                act.copy(xsT, ps[0:D, BANK_XST, :]).then_inc(xsT_copied, 1)

            def copy_yT(J):
                act.wait_ge(p1_done, NU * J)
                act.copy(yT[:, :], ps[:, BANK_YT, 0:W]).then_inc(yT_copied, 1)

            def keep_tiles(J, peeled):
                for g in range(NG):
                    for half in range(2):
                        if peeled and half and g + 2 < NG:
                            copy_xsT(g + 2)
                        u = 2 * (NG * J + g) + half
                        act.wait_ge(t_done, u + 1)
                        if not peeled and half == 0 and g not in DOUBLE:
                            act.wait_ge(p2_done, NG * (J - 1) + g + 1)
                        b0 = BANK_T + 2 * half
                        dst = AT[:, slot_of(J, g), :, :, half * 2 * P:(half + 1) * 2 * P]
                        act.copy(dst.rearrange("p h k (r i) -> p r (h k) i", r=2),
                                 ps[:, b0:b0 + 2, :].rearrange("p r (q i) -> p r q i", i=P)).then_inc(at_ready, 1)

            copy_xsT(0)
            copy_xsT(1)
            keep_tiles(0, True)
            with act.Fori(1, NB) as J:
                copy_yT(J)
                keep_tiles(J, False)
            copy_yT(NB)

            for i in range(ROUNDS):
                if 3 <= i < NG + 3:
                    g = i - 3
                    act.wait_ge(x1_turned, g + 1)
                    if g >= 1:
                        act.wait_ge(hid_mm, g)
                    act.copy(xT[:, :], ps[0:D, BANK_X1T, :]).then_inc(xT_copied, 1)
                if i < NG:
                    act.wait_ge(h_centred, i + 1)
                    if i == 0:
                        act.wait_ge(eps_set, 2)
                    else:
                        act.wait_ge(sq1_summed, i)
                    hv = ps[:, BANK_H + i % 2, :].rearrange("p (t w d) -> p t w d", w=2, d=D)
                    act.square(sq[:, 0, :, 0:D], hv[:, :, 0, :]).then_inc(sq1_made, 1)
                if 1 <= i < NG + 1:
                    g = i - 1
                    act.wait_ge(a_centred, g + 1)
                    if g >= 1:
                        act.wait_ge(sq2_summed, g)
                    act.square(sq[:, 1, :, 0:D], a[:, g % 2, :, :]).then_inc(sq2_made, 1)
                if 3 <= i < NG + 3:
                    g = i - 3
                    tiles = slice(g * G, (g + 1) * G)
                    zv = ps[:, BANK_Z, 0:G * D].rearrange("p (t d) -> p t d", d=D)
                    act.wait_ge(z_mm, g + 1)
                    act.copy(stat[:, tiles, 0:D], zv).then_inc(z_hi, 1)
                    act.copy(Z[:, tiles, :], zv).then_inc(z_copied, 1)
                    act.wait_ge(hid_mm, g + 1)
                    if g == 0:
                        act.wait_ge(hb_made, 1)
                    else:
                        act.wait_ge(u_mm, g)
                    act.activation(hid[:, :], ps[:, BANK_HID, :], ACT.Tanh, bias=hbias[:, 0:1]).then_inc(hid_made, 1)

            def copy_acc(m):
                act.wait_ge(p3_done, T * m)
                act.copy(accT[:, :], acc(m - 1)).then_inc(acc_copied, 1)

            def split_hi(m, peeled):
                for k in range(T):
                    v = T * m + k
                    act.wait_ge(t2_done, v + 1)
                    if not peeled or k >= STAGE:
                        act.wait_ge(p3_done, v - STAGE + 1)
                    act.copy(s_hi[:, k % STAGE, :], ps[:, BANK_T + k % TB, :]).then_inc(hi2_ready, 1)
                    if k == LAG and not peeled:
                        copy_acc(m)
                    if k % KP in SUM_AFTER:
                        c, r = k // KP, SUM_AFTER.index(k % KP)
                        if r == 0:
                            act.wait_ge(raw2_in[c], 16 * (m + 1))
                            if not peeled or c:
                                act.wait_ge(act_summed, PIECES * m + c)
                        ins = act.activation(dump[:, r, :], raw2[:, c, r, FOLD:PW], ACT.Copy,
                                             accum_out=rsp[:, bass.ds(m * G + r, 1), PIECES + c])
                        if r == G - 1:
                            ins.then_inc(act_summed, 1)

            split_hi(0, True)
            with act.Fori(1, NG) as m:
                split_hi(m, False)
            copy_acc(NG)

        @block.gpsimd
        def _(pool):
            pool.memset(ident[:, :], 0.0).then_inc(id_zero, 1)
            pool.wait_ge(id_zero, 1)
            pool.affine_select(out=ident[:, :], in_=ident[:, :], compare_op=ALU.not_equal, fill=1.0, base=0,
                               pattern=[[-1, P]], channel_multiplier=1).then_inc(id_made, 1)
            pool.wait_ge(id_made, 1)
            pool.tensor_tensor(add_halves[:, :], ident[:, 0:D], ident[:, D:2 * D], ALU.add).then_inc(add_made, 1)
            pool.memset(minus_half[:, :], -0.5).then_inc(half_made, 1)
            pool.memset(hT[:, SCRATCH:N], 0.0).then_inc(hT_zeroed, 1)

            def split_lo(J, u):
                half = u % 2
                pool.wait_ge(hi_ready, NU * J + u + 1)
                pool.tensor_tensor(nat_lo[:, u % NAT, 1, :], raw[:, u // 2 % RAW, half * U + 1, :],
                                   nat_hi[:, u % NAT, 1, :].bitcast(F32), ALU.subtract).then_inc(lo_pool, 1)

            for u in range(NU):
                split_lo(0, u)
                if u % 2:
                    g = u // 2
                    xg = X[:, g * G:(g + 1) * G, :]
                    pool.wait_ge(e_made, g + 1)
                    pool.tensor_tensor(xg, xg, xg, ALU.add).then_inc(x_doubled, 1)
                    pool.wait_ge(x_doubled, g + 1)
                    pool.tensor_tensor(xg, xg, bet[:, :].unsqueeze(1).to_broadcast([P, G, D]), ALU.add).then_inc(base_made, 1)
            with pool.Fori(1, NB) as J:
                for u in range(NU):
                    split_lo(J, u)

            pool.wait_ge(p1_done, NB * NU)
            pool.wait_ge(base_made, NG)
            pool.wait_ge(half_made, 1)
            pool.memset(sq[:, :, :, :], LN_EPS * D).then_inc(eps_set, 1)
            pool.memset(osq[:, :, D], LN_EPS * D).then_inc(eps_set, 1)

            def rstd_of(ln, ready):
                pool.tensor_tensor(rstd[:, ln, :], sqsum[:, ln, :], minus_half[:, :], ALU.pow).then_inc(ready, 1)

            for i in range(NG + 2):
                if i >= 2:
                    g = i - 2
                    pool.wait_ge(x1_ready, g + 1)
                    pool.tensor_tensor(R[:, g * G:(g + 1) * G, :], x1[:, g % 2, :, :],
                                       b2r[:, :].unsqueeze(1).to_broadcast([P, G, D]), ALU.add).then_inc(x1b_made, 1)
                if i < NG:
                    pool.wait_ge(sq1_summed, i + 1)
                    rstd_of(0, rstd1_ready)
                if 1 <= i < NG + 1:
                    pool.wait_ge(sq2_summed, i)
                    rstd_of(1, rstd2_ready)

            def rstd_of_out(m):
                pool.wait_ge(epi_link, EPI * m + EPI - 1)
                pool.tensor_tensor(ost[:, 2, :], ost[:, 1, :], minus_half[:, 0:G], ALU.pow).then_inc(orstd_ready, 1)

            def fold(m, peeled):
                for c in range(PIECES):
                    if not peeled and c == 2:
                        rstd_of_out(m - 1)
                    n = PIECES * m + c
                    q = FOLD // 2
                    pool.wait_ge(raw2_in[c], 16 * (m + 1))
                    if not peeled or c:
                        pool.wait_ge(fold_summed, n)
                    pool.tensor_tensor(f1[:, :, :], raw2[:, c, :, 0:q], raw2[:, c, :, q:2 * q], ALU.add).then_inc(fold1, 1)
                    pool.wait_ge(fold1, n + 1)
                    q //= 2
                    pool.tensor_tensor(f1[:, :, 0:q], f1[:, :, 0:q], f1[:, :, q:2 * q], ALU.add).then_inc(fold2, 1)
                    pool.wait_ge(fold2, n + 1)
                    q //= 2
                    pool.tensor_tensor(f1[:, :, 0:q], f1[:, :, 0:q], f1[:, :, q:2 * q], ALU.add).then_inc(fold3, 1)

            fold(0, True)
            with pool.Fori(1, NG) as m:
                fold(m, False)
            rstd_of_out(NG - 1)

        @block.vector
        def _(dve):
            dve.wait_ge(id_made, 1)
            dve.tensor_copy(ident_r[:, :], ident[:, :]).then_inc(id_round, 1)
            dve.wait_ge(e_consts_in, 16 * E_CONSTS)
            dve.tensor_tensor(pp[:, :], pars[:, 0:4:2], pars[:, 1:4:2], ALU.mult).then_inc(pp_made, 1)
            dve.wait_ge(diag_turned, 1)
            dve.tensor_copy(diag[:, :], ps[:, BANK_E, 0:T]).then_inc(diag_made, 1)
            dve.wait_ge(diag_made, 1)

            def scale_x(g):
                if g * G in [0] + X_PARTS:
                    dve.wait_ge(x_in[([0] + X_PARTS).index(g * G)], 16)
                if g >= 2:
                    dve.wait_ge(xs_turned, g - 1)
                dve.tensor_tensor(xs[:, g % 2, :, :], X[:, g * G:(g + 1) * G, :],
                                  diag[:, g * G:(g + 1) * G].unsqueeze(2).to_broadcast([P, G, D]),
                                  ALU.mult).then_inc(xs_made, 1)

            def make_e(g):
                who = 0 if g * G < UT else 1
                dve.wait_ge(e_mm, g + 1)
                if g == 0:
                    dve.wait_ge(pp_made, 1)
                else:
                    dve.wait_ge(e_made, g)
                dve.scalar_tensor_tensor(ef, ps[:, BANK_E, 0:G * D], pp[:, who:who + 1],
                                         X[:, g * G:(g + 1) * G, :].rearrange("p t d -> p (t d)"),
                                         ALU.mult, ALU.add).then_inc(e_sum, 1)
                dve.wait_ge(e_sum, g + 1)
                dst = stat[:, g * G:(g + 1) * G, :]
                ev = ef.rearrange("p (t d) -> p t d", d=D)
                dve.tensor_copy(dst[:, :, 0:D], ev).then_inc(e_hi, 1)
                dve.wait_ge(e_hi, g + 1)
                dve.tensor_tensor(dst[:, :, D:2 * D], ev, dst[:, :, 0:D].bitcast(F32), ALU.subtract).then_inc(e_made, 1)

            scale_x(0)
            scale_x(1)

            def split(J, u, peeled):
                n = NU * J + u
                g, half = u // 2, u % 2
                s = g % RAW
                if half == 0:
                    dve.wait_ge(raw_in[s], 16 * (NG // RAW * J + g // RAW + 1))
                if not peeled or u >= NAT:
                    dve.wait_ge(p1_done, n - NAT + 1)
                dve.tensor_copy(nat_hi[:, u % NAT, :, :], raw[:, s, half * U:(half + 1) * U, :]).then_inc(hi_ready, 1)
                dve.wait_ge(hi_ready, n + 1)
                dve.tensor_tensor(nat_lo[:, u % NAT, 0, :], raw[:, s, half * U, :], nat_hi[:, u % NAT, 0, :].bitcast(F32),
                                  ALU.subtract).then_inc(lo_dve, 1)

            def make_y(J):
                dve.wait_ge(y_turned, J)
                yv = ps[:, BANK_Y, 0:CH * D].rearrange("p (k d) -> p k d", d=D)
                dve.tensor_copy(ystat[:, :, 0:D], yv).then_inc(y_hi, 1)
                dve.wait_ge(y_hi, J)
                dve.tensor_tensor(ystat[:, :, D:2 * D], yv, ystat[:, :, 0:D].bitcast(F32), ALU.subtract).then_inc(y_ready, 1)

            def add_h(J, g):
                dve.wait_ge(p2_done, NG * (J - 1) + g + 1)
                cols = hT[:, g * G * P:(g + 1) * G * P]
                dve.tensor_tensor(cols, cols, ps[:, BANK_P2 + g % 2, :], ALU.add).then_inc(h_added, 1)

            def make_consts():
                dve.wait_ge(consts_in, 16 * CONSTS)
                dve.scalar_tensor_tensor(hbias[:, :], w1t[:, :], tc[:, 0:1], b1c[:, :], ALU.mult, ALU.add).then_inc(hb_made, 1)
                dve.wait_ge(add_made, 1)
                dve.tensor_scalar(centre[:, 0, :], add_halves[:, :], -1.0 / D, None, ALU.add).then_inc(centre_made, 1)
                dve.wait_ge(centre_made, 1)
                dve.tensor_tensor(centre[:, 1, :], centre[:, 0, :], gam[:, :], ALU.mult).then_inc(centre_made, 1)

            split(0, 0, True)
            split(0, 1, True)
            make_e(0)
            scale_x(2)
            split(0, 2, True)
            split(0, 3, True)
            for g in range(NG - 1):
                make_e(g + 1)
                if g == NG // 2:
                    make_consts()
                if g + 3 < NG:
                    scale_x(g + 3)
                if g + 2 == NG:
                    dve.wait_ge(e_made, NG)
                    dve.memset(hT[:, 0:SCRATCH], 0.0).then_inc(scratch_zeroed, 1)
                for u in (2 * g + 4, 2 * g + 5):
                    if u < NU:
                        split(0, u, True)
            dve.wait_ge(B_turned, 1)
            dve.tensor_copy(BTs[:, :], ps[0:D, BANK_E, 0:D]).then_inc(BT_made, 1)
            dve.wait_ge(hT_zeroed, 1)
            dve.wait_ge(scratch_zeroed, 1)

            def block_work(J, first):
                for u in range(NU):
                    split(J, u, False)
                    if not first:
                        for g in ADD_LATE_AFTER.get(u, []):
                            add_h(J - 1, g)
                    if u == MAKE_Y_AFTER:
                        make_y(J)
                    for g in ADD_AFTER.get(u, []):
                        add_h(J, g)

            block_work(1, True)
            with dve.Fori(2, NB) as J:
                block_work(J, False)
            for late in ADD_LATE_AFTER.values():
                for g in late:
                    add_h(NB - 1, g)
            make_y(NB)

            def inner_sum(dst, src):
                return dve.tensor_reduce(dst, src, AX.X, ALU.add)

            wide = [P, G, D]

            add_h(NB, 0)
            for i in range(ROUNDS):
                if 1 <= i < NG + 1:
                    g = i - 1
                    ag = a[:, g % 2, :, :]
                    hv = ps[:, BANK_H + g % 2, :].rearrange("p (t w d) -> p t w d", w=2, d=D)
                    dve.wait_ge(rstd1_ready, g + 1)
                    if g >= 2:
                        dve.wait_ge(x1_ready, g - 1)
                    dve.scalar_tensor_tensor(ag, hv[:, :, 1, :], RSTD_SCALE,
                                             rstd[:, 0, :].unsqueeze(2).to_broadcast(wide),
                                             ALU.mult, ALU.mult).then_inc(h_scaled, 1)
                    dve.wait_ge(h_scaled, g + 1)
                    dve.tensor_tensor(ag, ag, X[:, g * G:(g + 1) * G, :], ALU.add).then_inc(a_ready, 1)
                if i >= 4:
                    g = i - 4
                    tiles = slice(g * G, (g + 1) * G)
                    dve.wait_ge(z_copied, g + 1)
                    dve.tensor_tensor(stat[:, tiles, D:2 * D], ps[:, BANK_Z, 0:G * D].rearrange("p (t d) -> p t d", d=D),
                                      stat[:, tiles, 0:D].bitcast(F32), ALU.subtract).then_inc(z_ready, 1)
                if 1 <= i < NG + 1:
                    dve.wait_ge(a_ready, i)
                    inner_sum(sums[:, :], ag).then_inc(a_summed, 1)
                if 2 <= i < NG + 2:
                    g = i - 2
                    dve.wait_ge(rstd2_ready, g + 1)
                    if g >= 2:
                        dve.wait_ge(x1b_made, g - 1)
                        dve.wait_ge(x1_turned, g - 1)
                    dve.scalar_tensor_tensor(x1[:, g % 2, :, :], a[:, g % 2, :, :], -RSTD_SCALE,
                                             rstd[:, 1, :].unsqueeze(2).to_broadcast(wide),
                                             ALU.mult, ALU.mult).then_inc(x1_ready, 1)
                if 1 <= i < NG + 1:
                    dve.wait_ge(a_summed, i)
                    dve.scalar_tensor_tensor(ag, sums[:, :].unsqueeze(2).to_broadcast(wide), 1.0 / D, ag,
                                             ALU.mult, ALU.subtract).then_inc(a_centred, 1)
                if i + 1 < NG:
                    add_h(NB, i + 1)
                if i < NG:
                    dve.wait_ge(sq1_made, i + 1)
                    inner_sum(sqsum[:, 0, :], sq[:, 0, :, :]).then_inc(sq1_summed, 1)
                if i >= 4:
                    g = i - 4
                    dve.wait_ge(u_mm, g + 1)
                    dve.wait_ge(x1b_made, g + 1)
                    rg = R[:, g * G:(g + 1) * G, :]
                    dve.tensor_tensor(rg, rg, ps[:, BANK_U, 0:G * D].rearrange("p (t d) -> p t d", d=D),
                                      ALU.add).then_inc(r_ready, 1)
                if 1 <= i < NG + 1:
                    dve.wait_ge(sq2_made, i)
                    inner_sum(sqsum[:, 1, :], sq[:, 1, :, :]).then_inc(sq2_summed, 1)

            def epilogue(m, s):
                if s:
                    dve.wait_ge(epi_link, EPI * m + s)
                rows = bass.ds(m * G, G)
                if s == 0:
                    dve.wait_ge(fold_summed, PIECES * (m + 1))
                    dve.wait_ge(act_summed, PIECES * (m + 1))
                    ins = inner_sum(rst[:, :], rsp[:, rows, :])
                elif s == 1:
                    ins = dve.tensor_tensor(oz[:, :, :], Z[:, rows, :], rst[:, :].unsqueeze(2).to_broadcast(wide), ALU.mult)
                elif s == 2:
                    ins = dve.tensor_tensor(o[:, :, :], R[:, rows, :], oz[:, :, :], ALU.subtract)
                elif s in (3, 4):
                    dve.wait_ge(o_turned, m + 1)
                    half = ps[:, BANK_OUT, :].rearrange("p (r c) -> p r c", c=P)[:, :, (s - 3) * D:(s - 2) * D]
                    ins = dve.tensor_tensor(o[:, :, :], o[:, :, :], half, ALU.add)
                elif s == 5:
                    ins = inner_sum(ost[:, 0, :], o[:, :, :])
                elif s == 6:
                    ins = dve.scalar_tensor_tensor(o[:, :, :], ost[:, 0, :].unsqueeze(2).to_broadcast(wide), 1.0 / D,
                                                   o[:, :, :], ALU.mult, ALU.subtract)
                elif s == 7:
                    ins = dve.tensor_tensor(osq[:, :, 0:D], o[:, :, :], o[:, :, :], ALU.mult)
                elif s == 8:
                    ins = inner_sum(ost[:, 1, :], osq[:, :, :])
                else:
                    dve.wait_ge(orstd_ready, m + 1)
                    ins = dve.scalar_tensor_tensor(R[:, rows, :], o[:, :, :], -RSTD_SCALE,
                                                   ost[:, 2, :].unsqueeze(2).to_broadcast(wide), ALU.mult, ALU.mult)
                ins.then_inc(epi_link, 1)

            def split_lo(m, peeled):
                for k in range(T):
                    v = T * m + k
                    dve.wait_ge(hi2_ready, v + 1)
                    dve.tensor_tensor(s_lo[:, k % STAGE, :], ps[:, BANK_T + k % TB, :],
                                      s_hi[:, k % STAGE, :].bitcast(F32), ALU.subtract).then_inc(lo2_ready, 1)
                    if not peeled and k in EPI_AT:
                        epilogue(m - 1, EPI_AT.index(k))
                    if k % KP == KP - 1:
                        c = k // KP
                        dve.wait_ge(fold3, PIECES * m + c + 1)
                        inner_sum(rsp[:, bass.ds(m * G, G), c], f1[:, :, 0:FOLD // 8]).then_inc(fold_summed, 1)

            split_lo(0, True)
            with dve.Fori(1, NG) as m:
                split_lo(m, False)
            for s in range(EPI):
                epilogue(NG - 1, s)

        @block.tensor
        def _(pe):
            pe.wait_ge(id_made, 1)
            pe.wait_ge(e_consts_in, 16 * E_CONSTS)
            pe.transpose(ps[:, BANK_E, 0:T], diag_rows[:, :], ident[0:T, 0:T]).then_inc(diag_turned, 1)

            def turn_xs(g):
                pe.wait_ge(xs_made, g + 1)
                if g:
                    pe.wait_ge(xsT_copied, g)
                for r in range(G):
                    ins = pe.transpose(ps[0:D, BANK_XST, r * P:(r + 1) * P], xs[:, g % 2, r, :], ident[:, :])
                ins.then_inc(xs_turned, 1)

            def mm_e(g):
                pe.wait_ge(xsT_copied, g + 1)
                if g:
                    pe.wait_ge(e_sum, g)
                else:
                    pe.wait_ge(diag_made, 1)
                w = wu if g * G < UT else wi
                for r in range(G):
                    ins = pe.matmul(ps[:, BANK_E, r * D:(r + 1) * D], xsT[:, r * P:(r + 1) * P], w[:, :],
                                    start=True, stop=True)
                ins.then_inc(e_mm, 1)

            turn_xs(0)
            mm_e(0)
            turn_xs(1)

            def turn_tiles(J, u, peeled):
                n = NU * J + u
                pe.wait_ge(lo_dve, n + 1)
                pe.wait_ge(lo_pool, n + 1)
                if not peeled or u >= 2:
                    pe.wait_ge(at_ready, n - 1)
                for r in range(U):
                    for h, part in enumerate((nat_hi, nat_lo)):
                        for k in range(CH):
                            q = h * CH + k
                            ins = pe.transpose(ps[:, BANK_T + u % 2 * U + r, q * P:(q + 1) * P].bitcast(F32R),
                                               part[:, u % NAT, r, k * P:(k + 1) * P], ident_r[:, :])
                ins.then_inc(t_done, 1)

            def mm_y(u):
                for r in range(U):
                    i = u * U + r
                    for part in (nat_hi, nat_lo):
                        ins = pe.matmul(ps[:, BANK_YT, 0:W], stat[:, i, :], part[:, u % NAT, r, :],
                                        start=(i == 0 and part is nat_hi), stop=(i == T - 1 and part is nat_lo))
                ins.then_inc(p1_done, 1)

            def turn_y(J):
                pe.wait_ge(yT_copied, J)
                for k in range(CH):
                    ins = pe.matmul(ps[:, BANK_Y, k * D:(k + 1) * D], yT[:, k * P:(k + 1) * P], add_halves[:, :],
                                    start=True, stop=True)
                ins.then_inc(y_turned, 1)

            def mm_h(J, g):
                if g == 0:
                    pe.wait_ge(y_ready, J)
                pe.wait_ge(at_ready, 2 * (NG * (J - 1) + g + 1))
                if g >= 2:
                    pe.wait_ge(h_added, NG * (J - 1) + g - 1)
                for k in range(CH):
                    for h in range(2):
                        ins = pe.matmul(ps[:, BANK_P2 + g % 2, :], ystat[:, k, :], AT[:, slot_of(J - 1, g), h, k, :],
                                        start=(k == 0 and h == 0), stop=(k == CH - 1 and h == 1))
                ins.then_inc(p2_done, 1)

            def block_products(J):
                for u in range(NU):
                    if u // 2 in ALONE:
                        turn_tiles(J, u, False)
                    elif u % 2 == 0:
                        turn_tiles(J, u, False)
                        if u == 0:
                            turn_y(J)
                        turn_tiles(J, u + 1, False)
                    mm_y(u)
                    for g in P2_AFTER.get(u, []):
                        mm_h(J, g)

            pe.wait_ge(id_round, 1)
            for g in range(NG):
                if g == 0:
                    turn_tiles(0, 0, True)
                if g + 1 < NG:
                    mm_e(g + 1)
                if g:
                    turn_tiles(0, 2 * g, True)
                pe.wait_ge(e_made, g + 1)
                mm_y(2 * g)
                if g + 2 < NG:
                    turn_xs(g + 2)
                elif g + 1 == NG:
                    pe.wait_ge(consts_in, 16 * CONSTS)
                    pe.transpose(ps[0:D, BANK_E, 0:D], Bs[:, :], ident[0:D, 0:D]).then_inc(B_turned, 1)
                turn_tiles(0, 2 * g + 1, True)
                mm_y(2 * g + 1)
            pe.wait_ge(centre_made, 2)
            pe.wait_ge(BT_made, 1)
            with pe.Fori(1, NB) as J:
                block_products(J)
            turn_y(NB)

            def centre_h(g):
                pe.wait_ge(h_added, NG * (NB - 1) + g + 1)
                if g >= 2:
                    pe.wait_ge(h_scaled, g - 1)
                elif g == 0:
                    pe.wait_ge(at_ready, NB * NU)
                for r in range(G):
                    i = g * G + r
                    ins = pe.matmul(ps[:, BANK_H + g % 2, r * P:(r + 1) * P], hT[:, i * P:(i + 1) * P],
                                    centre[:, :, :].rearrange("p w d -> p (w d)"), start=True, stop=True)
                ins.then_inc(h_centred, 1)

            def turn_x1(g):
                pe.wait_ge(x1_ready, g + 1)
                if g:
                    pe.wait_ge(xT_copied, g)
                for r in range(G):
                    ins = pe.transpose(ps[0:D, BANK_X1T, r * P:(r + 1) * P], x1[:, g % 2, r, :], ident[:, :])
                ins.then_inc(x1_turned, 1)

            def mm_z(g):
                pe.wait_ge(xT_copied, g + 1)
                if g:
                    pe.wait_ge(z_copied, g)
                    pe.wait_ge(z_ready, g)
                for r in range(G):
                    ins = pe.matmul(ps[:, BANK_Z, r * D:(r + 1) * D], xT[:, r * P:(r + 1) * P], BTs[:, :],
                                    start=True, stop=True)
                ins.then_inc(z_mm, 1)
                if g:
                    pe.wait_ge(hid_made, g)
                pe.matmul(ps[:, BANK_HID, :], w1[:, :], xT[:, :], start=True, stop=True).then_inc(hid_mm, 1)

            def mm_u(g):
                pe.wait_ge(hid_made, g + 1)
                if g:
                    pe.wait_ge(r_ready, g)
                for r in range(G):
                    ins = pe.matmul(ps[:, BANK_U, r * D:(r + 1) * D], hid[:, r * P:(r + 1) * P], w2[:, :],
                                    start=True, stop=True)
                ins.then_inc(u_mm, 1)

            mm_h(NB, 0)
            mm_h(NB, 1)
            for i in range(ROUNDS):
                if 3 <= i < NG + 3:
                    turn_x1(i - 3)
                if i < NG:
                    centre_h(i)
                if i >= 4:
                    mm_u(i - 4)
                if i + 2 < NG:
                    mm_h(NB, i + 2)
                if 3 <= i < NG + 3:
                    mm_z(i - 3)

            def turn_chunk(m, k, peeled):
                v = T * m + k
                if k % KP == 0:
                    pe.wait_ge(raw2_in[k // KP], 16 * (m + 1))
                if not peeled or k >= TB:
                    pe.wait_ge(lo2_ready, v - TB + 1)
                for r in range(G):
                    ins = pe.transpose(ps[:, BANK_T + k % TB, r * P:(r + 1) * P],
                                       raw2[:, k // KP, r, (k % KP) * P:(k % KP + 1) * P], ident[:, :])
                ins.then_inc(t2_done, 1)

            def mm_az(m, k):
                pe.wait_ge(lo2_ready, T * m + k + 1)
                ins = pe.matmul(acc(m), stat[:, k, :], s_hi[:, k % STAGE, :], start=(k == 0), stop=False)
                if k % KP == KP - 1:
                    ins.then_inc(turned, 1)
                pe.matmul(acc(m), stat[:, k, :], s_lo[:, k % STAGE, :], start=False,
                          stop=(k == T - 1)).then_inc(p3_done, 1)

            def turn_out(m):
                pe.wait_ge(acc_copied, m)
                for r in range(G):
                    ins = pe.transpose(ps[:, BANK_OUT, r * P:(r + 1) * P], accT[:, r * P:(r + 1) * P], ident[:, :])
                ins.then_inc(o_turned, 1)

            def row_group(m, peeled):
                for k in range(T):
                    turn_chunk(m, k, peeled)
                    if k >= LAG:
                        mm_az(m, k - LAG)
                    elif not peeled:
                        mm_az(m - 1, T - LAG + k)
                    if k == LAG + 2 and not peeled:
                        turn_out(m)

            pe.wait_ge(hid_made, NG)
            pe.wait_ge(z_ready, NG)
            pe.wait_ge(z_copied, NG)
            pe.wait_ge(r_ready, NG)
            row_group(0, True)
            with pe.Fori(1, NG) as m:
                row_group(m, False)
            for k in range(T - LAG, T):
                mm_az(NG - 1, k)
            turn_out(NG)


_INS = ["x", "adj", "L0_gnn_W_u", "L0_gnn_diag_u", "L0_gnn_par_u", "L0_gnn_W_i", "L0_gnn_diag_i", "L0_gnn_par_i",
        "L0_gnn_ln_gamma", "L0_gnn_ln_beta", "L1_gnn_t", "L1_gnn_B", "L1_gnn_W1", "L1_gnn_b1", "L1_gnn_W2", "L1_gnn_b2"]


def kernel(**inputs):
    import numpy as _np
    import concourse.bacc as _bacc
    from concourse import mybir as _mybir
    from concourse.bass_utils import run_bass_kernel_spmd as _run

    nc = _bacc.Bacc("TRN2", target_bir_lowering=False, num_devices=1)
    arrays, args = {}, []
    for name in _INS:
        a = _np.ascontiguousarray(inputs[name])
        arrays[f"in_{name}_dram"] = a
        args.append(nc.dram_tensor(f"in_{name}_dram", a.shape, _mybir.dt.from_np(a.dtype), kind="ExternalInput").ap())
    args.append(nc.dram_tensor("out_0_dram", (N, D), F32, kind="ExternalOutput").ap())
    build(nc, *args)
    r = _run(nc, [arrays], core_ids=[0])
    return r.results[0]["out_0_dram"]
```
